# Optimizing a Trainium2 kernel written in Bass

```python
import numpy as np
import jax
import jax.numpy as jnp

def _softmax(x, axis=-1):
    return jax.nn.softmax(x, axis=axis)

def _gelu(x):
    return jax.nn.gelu(x, approximate=True)

def _silu(x):
    return jax.nn.silu(x)

def _sigmoid(x):
    return jax.nn.sigmoid(x)

def _layernorm(x, axis=-1, eps=1e-05):
    m = jnp.mean(x, axis=axis, keepdims=True)
    v = jnp.var(x, axis=axis, keepdims=True)
    return (x - m) / jnp.sqrt(v + eps)

def _scatter_add(tgt, idx, src, axis=0):
    return tgt.at[idx].add(src)

def _segment_sum(src, seg, n):
    return jax.ops.segment_sum(src, seg, n)
kernel_name = 'mk_adaln_d1_jaxref_r2_014875'

def setup_inputs(seed: int=0):
    np.random.seed(seed)
    _w = jnp.asarray

    def _L0_attn_setup():
        import jax, jax.numpy as jnp
        import numpy as np
        D_MODEL = 512
        N_LAYERS = 2
        D_STATE = 64
        D_CONV = 4
        EXPAND = 2
        D_INNER = EXPAND * D_MODEL
        HEADDIM = D_STATE
        NHEADS = D_INNER // HEADDIM
        CONV_DIM = D_INNER + 2 * D_STATE
        D_IN_PROJ = 2 * D_INNER + 2 * D_STATE + NHEADS
        EPS = 1e-05

        def _layernorm(x, w, b):
            m = x.mean(-1, keepdims=True)
            v = ((x - m) ** 2).mean(-1, keepdims=True)
            return (x - m) * jax.lax.rsqrt(v + EPS) * w + b

        def _mamba2(u, in_w, conv_w, conv_b, dt_bias, A_log, Dp, rms_w, out_w):
            b, l, _ = u.shape
            zxbcdt = u @ in_w.T
            z, xBC, dt = jnp.split(zxbcdt, [D_INNER, D_INNER + CONV_DIM], axis=-1)
            dt = jax.nn.softplus(dt + dt_bias)
            xBC = jnp.transpose(xBC, (0, 2, 1))
            xBC = jax.lax.conv_general_dilated(xBC, conv_w[:, None, :], (1,), [(D_CONV - 1, 0)], dimension_numbers=('NCH', 'OIH', 'NCH'), feature_group_count=CONV_DIM)
            xBC = jnp.transpose(xBC, (0, 2, 1)) + conv_b
            xBC = jax.nn.silu(xBC)
            xh, Bm, Cm = jnp.split(xBC, [D_INNER, D_INNER + D_STATE], axis=-1)
            xh = xh.reshape(b, l, NHEADS, HEADDIM)
            A = -jnp.exp(A_log)
            dA = jnp.exp(dt * A)

            def step(state, inputs):
                dA_t, dt_t, x_t, B_t, C_t = inputs
                state = dA_t[:, :, None, None] * state + (dt_t[:, :, None] * x_t)[..., None] * B_t[:, None, None, :]
                y_t = jnp.einsum('bhpn,bn->bhp', state, C_t)
                return (state, y_t)
            xs = (jnp.moveaxis(dA, 1, 0), jnp.moveaxis(dt, 1, 0), jnp.moveaxis(xh, 1, 0), jnp.moveaxis(Bm, 1, 0), jnp.moveaxis(Cm, 1, 0))
            init = jnp.zeros((b, NHEADS, HEADDIM, D_STATE), u.dtype)
            _, ys = jax.lax.scan(step, init, xs)
            y = jnp.moveaxis(ys, 0, 1) + Dp[None, None, :, None] * xh
            y = y.reshape(b, l, D_INNER)
            y = y * jax.nn.silu(z)
            y = y * jax.lax.rsqrt(jnp.mean(y * y, -1, keepdims=True) + EPS) * rms_w
            return y @ out_w.T
        key = jax.random.key(seed)
        ks = jax.random.split(key, 8)
        B, L = (2, 2048)
        return {'x': jax.random.normal(ks[0], (B, L, D_MODEL), jnp.float32), 'ln_w': jnp.ones((N_LAYERS, D_MODEL), jnp.float32), 'ln_b': jnp.zeros((N_LAYERS, D_MODEL), jnp.float32), 'in_proj_w': jax.random.normal(ks[1], (N_LAYERS, D_IN_PROJ, D_MODEL), jnp.float32) * D_MODEL ** (-0.5), 'conv_w': jax.random.normal(ks[2], (N_LAYERS, CONV_DIM, D_CONV), jnp.float32) * D_CONV ** (-0.5), 'conv_b': jnp.zeros((N_LAYERS, CONV_DIM), jnp.float32), 'dt_bias': jax.random.normal(ks[3], (N_LAYERS, NHEADS), jnp.float32) * 0.5, 'A_log': jnp.log(jax.random.uniform(ks[4], (N_LAYERS, NHEADS), jnp.float32, 1.0, 16.0)), 'D': jnp.ones((N_LAYERS, NHEADS), jnp.float32), 'rms_w': jnp.ones((N_LAYERS, D_INNER), jnp.float32), 'out_proj_w': jax.random.normal(ks[5], (N_LAYERS, D_MODEL, D_INNER), jnp.float32) * D_INNER ** (-0.5)}
    _L0_attn_in = _L0_attn_setup()

    def _L0_ffn_setup():
        import jax, jax.numpy as jnp
        import numpy as np
        DIM = 512

        def _reference_tuple_inner(x, W_r, W_k, W_v, mu_r, mu_k):
            B, T, C = x.shape
            x_prev = jnp.concatenate([jnp.zeros((B, 1, C), x.dtype), x[:, :-1, :]], axis=1)
            xr = mu_r * x + (1.0 - mu_r) * x_prev
            xk = mu_k * x + (1.0 - mu_k) * x_prev
            r = jax.nn.sigmoid(jnp.einsum('btc,dc->btd', xr, W_r))
            k = jnp.einsum('btc,dc->btd', xk, W_k)
            k_act = jnp.square(jax.nn.relu(k))
            out = r * jnp.einsum('btc,dc->btd', k_act, W_v)
            new_state = x[:, -1, :]
            return (out, new_state)
        key = jax.random.key(seed)
        ks = jax.random.split(key, 6)
        B, T, C = (8, 1024, DIM)
        x = jax.random.normal(ks[0], (B, T, C), dtype=jnp.float32)
        s = 1.0 / np.sqrt(C)
        W_r = jax.random.uniform(ks[1], (C, C), jnp.float32, -s, s)
        W_k = jax.random.uniform(ks[2], (C, C), jnp.float32, -s, s)
        W_v = jax.random.uniform(ks[3], (C, C), jnp.float32, -s, s)
        mu_r = jax.random.uniform(ks[4], (C,), jnp.float32)
        mu_k = jax.random.uniform(ks[5], (C,), jnp.float32)
        return {'x': x, 'W_r': W_r, 'W_k': W_k, 'W_v': W_v, 'mu_r': mu_r, 'mu_k': mu_k}
    _L0_ffn_in = _L0_ffn_setup()
    _L0_c = _w((lambda *s: np.random.randn(*s).astype(np.float32) * 0.05)(8, 512))
    _L0_wmod = _w((lambda *s: np.random.randn(*s).astype(np.float32) * 0.05)(512, 6 * 512) * 512 ** (-0.5))
    _d = {'L0_attn_x': _L0_attn_in['x'], 'L0_attn_ln_w': _L0_attn_in['ln_w'], 'L0_attn_ln_b': _L0_attn_in['ln_b'], 'L0_attn_in_proj_w': _L0_attn_in['in_proj_w'], 'L0_attn_conv_w': _L0_attn_in['conv_w'], 'L0_attn_conv_b': _L0_attn_in['conv_b'], 'L0_attn_dt_bias': _L0_attn_in['dt_bias'], 'L0_attn_A_log': _L0_attn_in['A_log'], 'L0_attn_D': _L0_attn_in['D'], 'L0_attn_rms_w': _L0_attn_in['rms_w'], 'L0_attn_out_proj_w': _L0_attn_in['out_proj_w'], 'L0_ffn_W_r': _L0_ffn_in['W_r'], 'L0_ffn_W_k': _L0_ffn_in['W_k'], 'L0_ffn_W_v': _L0_ffn_in['W_v'], 'L0_ffn_mu_r': _L0_ffn_in['mu_r'], 'L0_ffn_mu_k': _L0_ffn_in['mu_k'], 'L0_c': _L0_c, 'L0_wmod': _L0_wmod}
    _x0 = _d['L0_attn_x']
    _d['L0_attn_x'] = jax.random.normal(jax.random.fold_in(jax.random.key(seed), 1), (8, 1024, 512), dtype=_x0.dtype)
    del _x0
    return _d

def reference(L0_attn_x, L0_attn_ln_w, L0_attn_ln_b, L0_attn_in_proj_w, L0_attn_conv_w, L0_attn_conv_b, L0_attn_dt_bias, L0_attn_A_log, L0_attn_D, L0_attn_rms_w, L0_attn_out_proj_w, L0_ffn_W_r, L0_ffn_W_k, L0_ffn_W_v, L0_ffn_mu_r, L0_ffn_mu_k, L0_c, L0_wmod):

    def _L0_attn_ref(x, ln_w, ln_b, in_proj_w, conv_w, conv_b, dt_bias, A_log, D, rms_w, out_proj_w):
        import jax, jax.numpy as jnp
        import numpy as np
        D_MODEL = 512
        N_LAYERS = 2
        D_STATE = 64
        D_CONV = 4
        EXPAND = 2
        D_INNER = EXPAND * D_MODEL
        HEADDIM = D_STATE
        NHEADS = D_INNER // HEADDIM
        CONV_DIM = D_INNER + 2 * D_STATE
        D_IN_PROJ = 2 * D_INNER + 2 * D_STATE + NHEADS
        EPS = 1e-05

        def _layernorm(x, w, b):
            m = x.mean(-1, keepdims=True)
            v = ((x - m) ** 2).mean(-1, keepdims=True)
            return (x - m) * jax.lax.rsqrt(v + EPS) * w + b

        def _mamba2(u, in_w, conv_w, conv_b, dt_bias, A_log, Dp, rms_w, out_w):
            b, l, _ = u.shape
            zxbcdt = u @ in_w.T
            z, xBC, dt = jnp.split(zxbcdt, [D_INNER, D_INNER + CONV_DIM], axis=-1)
            dt = jax.nn.softplus(dt + dt_bias)
            xBC = jnp.transpose(xBC, (0, 2, 1))
            xBC = jax.lax.conv_general_dilated(xBC, conv_w[:, None, :], (1,), [(D_CONV - 1, 0)], dimension_numbers=('NCH', 'OIH', 'NCH'), feature_group_count=CONV_DIM)
            xBC = jnp.transpose(xBC, (0, 2, 1)) + conv_b
            xBC = jax.nn.silu(xBC)
            xh, Bm, Cm = jnp.split(xBC, [D_INNER, D_INNER + D_STATE], axis=-1)
            xh = xh.reshape(b, l, NHEADS, HEADDIM)
            A = -jnp.exp(A_log)
            dA = jnp.exp(dt * A)

            def step(state, inputs):
                dA_t, dt_t, x_t, B_t, C_t = inputs
                state = dA_t[:, :, None, None] * state + (dt_t[:, :, None] * x_t)[..., None] * B_t[:, None, None, :]
                y_t = jnp.einsum('bhpn,bn->bhp', state, C_t)
                return (state, y_t)
            xs = (jnp.moveaxis(dA, 1, 0), jnp.moveaxis(dt, 1, 0), jnp.moveaxis(xh, 1, 0), jnp.moveaxis(Bm, 1, 0), jnp.moveaxis(Cm, 1, 0))
            init = jnp.zeros((b, NHEADS, HEADDIM, D_STATE), u.dtype)
            _, ys = jax.lax.scan(step, init, xs)
            y = jnp.moveaxis(ys, 0, 1) + Dp[None, None, :, None] * xh
            y = y.reshape(b, l, D_INNER)
            y = y * jax.nn.silu(z)
            y = y * jax.lax.rsqrt(jnp.mean(y * y, -1, keepdims=True) + EPS) * rms_w
            return y @ out_w.T
        h = x
        for i in range(N_LAYERS):
            res = h
            h = _layernorm(h, ln_w[i], ln_b[i])
            h = _mamba2(h, in_proj_w[i], conv_w[i], conv_b[i], dt_bias[i], A_log[i], D[i], rms_w[i], out_proj_w[i])
            h = h + res
        return h

    def _L0_ffn_ref(x, W_r, W_k, W_v, mu_r, mu_k):
        import jax, jax.numpy as jnp
        import numpy as np
        DIM = 512

        def _reference_tuple_inner(x, W_r, W_k, W_v, mu_r, mu_k):
            B, T, C = x.shape
            x_prev = jnp.concatenate([jnp.zeros((B, 1, C), x.dtype), x[:, :-1, :]], axis=1)
            xr = mu_r * x + (1.0 - mu_r) * x_prev
            xk = mu_k * x + (1.0 - mu_k) * x_prev
            r = jax.nn.sigmoid(jnp.einsum('btc,dc->btd', xr, W_r))
            k = jnp.einsum('btc,dc->btd', xk, W_k)
            k_act = jnp.square(jax.nn.relu(k))
            out = r * jnp.einsum('btc,dc->btd', k_act, W_v)
            new_state = x[:, -1, :]
            return (out, new_state)
        return _reference_tuple_inner(x, W_r, W_k, W_v, mu_r, mu_k)[0]
    x = L0_attn_x
    mod = (_silu(L0_c) @ L0_wmod).reshape(L0_c.shape[0], 6, 1, -1)
    sa, ca, ga, sb, cb, gb = (mod[:, 0], mod[:, 1], mod[:, 2], mod[:, 3], mod[:, 4], mod[:, 5])
    ga = (2 * (ga >= 0) - 1) * jnp.maximum(jnp.abs(ga), 0.25)
    gb = (2 * (gb >= 0) - 1) * jnp.maximum(jnp.abs(gb), 0.25)
    h = _layernorm(x, axis=-1) * (1 + ca) + sa
    x = x + ga * _L0_attn_ref(h, L0_attn_ln_w, L0_attn_ln_b, L0_attn_in_proj_w, L0_attn_conv_w, L0_attn_conv_b, L0_attn_dt_bias, L0_attn_A_log, L0_attn_D, L0_attn_rms_w, L0_attn_out_proj_w)
    h = _layernorm(x, axis=-1) * (1 + cb) + sb
    x = x + gb * _L0_ffn_ref(h, L0_ffn_W_r, L0_ffn_W_k, L0_ffn_W_v, L0_ffn_mu_r, L0_ffn_mu_k)
    return x

_drawn_inputs = setup_inputs


def setup_inputs(seed=0):
    import zlib

    import numpy as np

    out = dict(_drawn_inputs(seed))
    spreads = {'L0_attn_ln_w': (1.0, 0.2),
     'L0_attn_ln_b': (0.0, 0.1),
     'L0_attn_conv_b': (0.0, 0.1),
     'L0_attn_D': (1.0, 0.2),
     'L0_attn_rms_w': (1.0, 0.2)}
    factors = {'L0_ffn_W_r': 8.0,
     'L0_ffn_W_k': 3.332,
     'L0_ffn_W_v': 3.034,
     'L0_ffn_mu_r': 8.0,
     'L0_ffn_mu_k': 5.54}
    for name, (base, spread) in spreads.items():
        noise = np.random.default_rng([zlib.crc32(name.encode()), seed]).standard_normal(out[name].shape)
        drawn = base * np.exp(spread * noise) if base else spread * noise
        out[name] = jnp.asarray(drawn.astype(out[name].dtype))
    for name, factor in factors.items():
        out[name] = (out[name] * factor).astype(out[name].dtype)
    return out
```

```python
from contextlib import ExitStack

import numpy as np

import concourse.bass as bass
from concourse import mybir

ALU = mybir.AluOpType
ACT = mybir.ActivationFunctionType
F32 = mybir.dt.float32
F32R = mybir.dt.float32r

P = 128
DM = 512
DI = 1024
NS = 64
NH = DI // NS
NL = 2
KD = DM // P
KI = DI // P
CH = 64
TB = 256
NB = 4
NPAIR = TB // P
WIN = 2 * P + 2 * DI
TAPS = 4
NG = WIN // (2 * P)
NX = KI // 2
EPS = 1e-5
MINUS_BIG = -1e30

C_CW = 0
C_CB = C_CW + 9 * TAPS
C_D = C_CB + 9
C_RMS = C_D + KI
C_LNW = C_RMS + KI
C_LNB = C_LNW + KD
C_ALOG = C_LNB + KD
C_DTB = C_ALOG + 1
NPRM = C_DTB + 1

K_RHS = 0
K_LHS = K_RHS + NH * CH
K_ID = K_LHS + TB // CH * P
K_SCAN = K_ID + P
K_DELTA = K_SCAN + TB
K_LOW = K_DELTA + NH
K_ONE = K_LOW + 1
K_HALF = K_ONE + 1
K_EPS = K_HALF + 2
K_BLK = K_EPS + 2
NCST = K_BLK + 2


def shape_constants():
    c = np.zeros((P, NCST), np.float32)
    p = np.arange(P)
    h, t = np.arange(NH), np.arange(CH)
    rhs = np.zeros((P, NH, CH), np.float32)
    rhs[32:64] = (p[32:64, None] % NH == h[None, :])[:, :, None]
    rhs[64:] = np.where(t[None, :] < np.arange(CH)[:, None], MINUS_BIG, 0.0)[:, None, :]
    c[:, K_RHS:K_LHS] = rhs.reshape(P, -1)
    lhs = np.zeros((P, TB // CH, P), np.float32)
    lhs[0:32] = 1.0
    for k in range(TB // CH):
        tok = (k % 2) * CH
        lhs[64:, k, tok:tok + CH] = np.eye(CH, dtype=np.float32)
    c[:, K_LHS:K_ID] = lhs.reshape(P, -1)
    c[:, K_ID:K_SCAN] = np.eye(P, dtype=np.float32)
    c[:, K_SCAN:K_DELTA] = (np.arange(TB) % CH != 0)[None, :]
    c[:, K_DELTA:K_LOW] = p[:, None] % NH == h[None, :]
    c[:, K_LOW] = (p // NH) % 2
    c[:, K_ONE] = 1.0
    c[:, K_HALF:K_EPS] = -0.5
    c[:, K_EPS:K_BLK] = EPS
    c[:, K_BLK:NCST] = p[:, None] // CH == np.arange(2)[None, :]
    return c


def modulation(nc, sems, cT, wmod, cst, mod_dram, cols_dram, nseq):
    with ExitStack() as ctx:
        def sb(name, shape, dt=F32):
            return ctx.enter_context(nc.sbuf_tensor(name, shape, dt))

        def sem(name):
            return sems(name)

        c_sb = sb("m_c", [P, KD, nseq])
        sc_sb = sb("m_sc", [P, KD, nseq])
        w_sb = sb("m_w", [P, KD, 6 * DM])
        mod_sb = sb("m_mod", [nseq, 6, DM])
        mag_sb = sb("m_mag", [nseq, 6, DM])
        sgn_sb = sb("m_sgn", [nseq, 6, DM])
        id_sb = sb("m_id", [P, P])
        cols_sb = sb("m_cols", [P, nseq, 2 * KD])
        ps = ctx.enter_context(nc.psum_tensor("m_ps", [P, 6, DM], F32))
        ps_c = ctx.enter_context(nc.psum_tensor("m_psc", [P, 2 * KD, nseq], F32))
        turned, cols_done = sem("m_turned"), sem("m_cols_done")
        c_loaded, w_loaded, c_silu, mod_done = sem("m_cl"), sem("m_wl"), sem("m_silu"), sem("m_mm")
        copied, mag_done, sgn_done, post_done, stored = (
            sem("m_cp"), sem("m_mg"), sem("m_sg"), sem("m_post"), sem("m_st"))
        block = ctx.enter_context(nc.Block())

        @block.sync
        def _(sp):
            sp.dma_start(c_sb[:], cT).then_inc(c_loaded, 16)
            sp.dma_start(w_sb[:], wmod).then_inc(w_loaded, 16)
            sp.dma_start(id_sb[:], cst[:, K_ID:K_ID + P]).then_inc(w_loaded, 16)
            sp.wait_ge(post_done, 4)
            sp.dma_start(mod_dram.rearrange("b (s d) -> b s d", s=6), mod_sb[:]).then_inc(stored, 16)
            sp.wait_ge(cols_done, 1)
            sp.dma_start(cols_dram.rearrange("b p k -> p b k"), cols_sb[:]).then_inc(stored, 16)
            sp.wait_ge(stored, 32)

        @block.scalar
        def _(act):
            act.wait_ge(c_loaded, 16)
            nc.scalar.activation(sc_sb[:], c_sb[:], ACT.Silu).then_inc(c_silu, 1)

        @block.tensor
        def _(pe):
            pe.wait_ge(c_silu, 1)
            pe.wait_ge(w_loaded, 32)
            for n in range(6):
                for k in range(KD):
                    last = nc.tensor.matmul(ps[0:nseq, n, :], sc_sb[:, k, :], w_sb[:, k, n * DM:(n + 1) * DM],
                                            start=(k == 0), stop=(k == KD - 1))
            last.then_inc(mod_done, 1)
            pe.wait_ge(post_done, 4)
            for k in range(2 * KD):
                last = nc.tensor.transpose(ps_c[:, k, :], mod_sb[:, 3 + k // KD, (k % KD) * P:(k % KD + 1) * P],
                                           id_sb[0:nseq, 0:nseq])
            last.then_inc(turned, 1)

        @block.vector
        def _(dve):
            dve.wait_ge(mod_done, 1)
            nc.vector.tensor_copy(mod_sb[:], ps[0:nseq]).then_inc(copied, 1)
            dve.wait_ge(copied, 1)
            for n in (1, 4):
                nc.vector.tensor_scalar_add(mod_sb[:, n, :], mod_sb[:, n, :], 1.0).then_inc(post_done, 1)
            for k, n in enumerate((2, 5)):
                g = mod_sb[:, n, :]
                nc.vector.tensor_scalar_mul(mag_sb[:, n, :], g, -1.0).then_inc(mag_done, 1)
                nc.vector.tensor_scalar(sgn_sb[:, n, :], g, 0.0, 2.0, ALU.is_ge, ALU.mult).then_inc(sgn_done, 1)
                dve.wait_ge(mag_done, 3 * k + 1)
                nc.vector.tensor_tensor(mag_sb[:, n, :], mag_sb[:, n, :], g, ALU.max).then_inc(mag_done, 1)
                dve.wait_ge(mag_done, 3 * k + 2)
                nc.vector.tensor_scalar_max(mag_sb[:, n, :], mag_sb[:, n, :], 0.25).then_inc(mag_done, 1)
                dve.wait_ge(mag_done, 3 * k + 3)
                dve.wait_ge(sgn_done, k + 1)
                nc.vector.scalar_tensor_tensor(out=g, in0=sgn_sb[:, n, :], scalar=-1.0, in1=mag_sb[:, n, :],
                                               op0=ALU.add, op1=ALU.mult).then_inc(post_done, 1)
            dve.wait_ge(turned, 1)
            nc.vector.tensor_copy(cols_sb[:].rearrange("p b k -> p k b"), ps_c[:]).then_inc(cols_done, 1)


def mamba_layer(nc, sems, layer, src, dst, in_w, out_w, prm, cst, mod_dram, nseq):
    first = layer == 0
    b0 = layer * nseq
    with ExitStack() as ctx:
        def sb(name, shape, dt=F32):
            return ctx.enter_context(nc.sbuf_tensor(f"l{layer}_{name}", shape, dt))

        def psum(name, shape):
            return ctx.enter_context(nc.psum_tensor(f"l{layer}_{name}", shape, F32))

        def sem(name):
            return sems("l_" + name)

        wi_hi, wi_lo = sb("wi_hi", [P, KD, WIN], F32R), sb("wi_lo", [P, KD, WIN], F32R)
        wo_hi, wo_lo = sb("wo_hi", [P, KI, DM], F32R), sb("wo_lo", [P, KI, DM], F32R)
        prm_sb = sb("prm", [P, NPRM])
        small = sb("small", [P, NCST - K_ID])
        a_neg = sb("a_neg", [P, 1])
        h_sb = sb("h", [P, 2, NPAIR, DM])
        hn = sb("hn", [P, NPAIR, DM])
        v = sb("v", [P, 2, TB])
        u_hi, u_lo = sb("u_hi", [P, KD, TB], F32R), sb("u_lo", [P, KD, TB], F32R)
        raw = sb("raw", [P, 2, TB + TAPS - 1])
        acc = sb("acc", [P, 2, TB])
        halo = sb("halo", [P, 9, TAPS - 1])
        xc = sb("xc", [P, KI, TB])
        zs = sb("zs", [P, KI, TB])
        bti = sb("bti", [NS, TB // CH, P])
        bt, ct = sb("bt", [NS, TB]), sb("ct", [NS, TB])
        dt = sb("dt", [P, TB])
        dtx = sb("dtx", [P, TB])
        dty = sb("dty", [P, TB])
        cum = sb("cum", [P, TB])
        chi = sb("chi", [P, TB], F32R)
        lhs = sb("lhs", [P, TB // CH, P], F32R)
        rhs = sb("rhs", [P, NH, CH], F32R)
        misc = sb("misc", [P, 4, 64])
        bd = sb("bd", [P, P])
        xs = sb("xs", [P, 2, DI])
        xw = sb("xw", [P, DI])
        e = sb("e", [P, 2, NH, CH])
        dec = sb("dec", [P, 2, NH])
        sd = sb("sd", [P, DI])
        g = sb("g", [P, KI, P])
        g_hi, g_lo = sb("g_hi", [P, KI, P], F32R), sb("g_lo", [P, KI, P], F32R)
        ms = sb("ms", [P, 1])
        rr = sb("rr", [P, 1])
        spare = sb("spare", [P, 1])
        stats = sb("stats", [P, NPAIR, 6])
        mv = sb("mv", [P, NPAIR, 2])
        rstd = sb("rstd", [P, NPAIR])
        if first:
            mod = sb("mod", [P, 2, DM])

        ring = psum("ring", [P, 2, 512])
        wide = psum("wide", [P, 2, DI])
        ps_y = psum("ps_y", [P, KI, CH])
        ps_m = psum("ps_m", [P, 512])

        rounds = 2 if first else 1

        def norm_round(i, rnd):
            return 2 * i + rnd if first else i + NB * nseq

        def const(a, n):
            return small[:, a - K_ID:a - K_ID + n]

        ident, one = const(K_ID, P), const(K_ONE, 1)
        ring_uses = 2 * NPAIR + NG

        s_cst, s_prm = sem("cst"), sem("prm")
        s_stage = [sem("stage0"), sem("stage1")]
        s_whi, s_wlo, s_wsc = sem("w_hi"), sem("w_lo"), sem("w_scaled")
        s_init, s_aexp, s_aneg, s_cst_copy = sem("init"), sem("a_exp"), sem("a_neg"), sem("cst_copy")
        s_load = [sem("load0"), sem("load1")]
        s_store = [sem("store0"), sem("store1")]
        s_mod = sem("mod")
        s_bn, s_mv, s_var, s_rstd, s_norm, s_modm, s_moda = (
            sem("bn"), sem("mv"), sem("var"), sem("rstd"), sem("norm"), sem("mod_mul"), sem("mod_add"))
        s_ut, s_utev, s_v, s_uhi, s_ulo = sem("u_T"), sem("u_T_read"), sem("v"), sem("u_hi"), sem("u_lo")
        s_in, s_inev = sem("proj"), sem("proj_read")
        s_xb, s_abs, s_exp, s_ln, s_dt = sem("dt_x"), sem("dt_abs"), sem("dt_exp"), sem("dt_ln"), sem("dt")
        s_a, s_cum, s_chi, s_vr, s_lhs, s_dend, s_wexp, s_td = (
            sem("dta"), sem("cum"), sem("cum_hi"), sem("cum_parts"), sem("lhs"), sem("d_end"), sem("w_exp"),
            sem("dt_w"))
        s_halo, s_raw, s_halo2, s_acc0, s_acc, s_bc, s_xc = (
            sem("halo"), sem("raw"), sem("halo2"), sem("acc0"), sem("acc"), sem("bc"), sem("xc"))
        s_tap = sem("tap")
        s_rhs, s_arg, s_e, s_dec, s_m = sem("rhs"), sem("arg"), sem("e"), sem("dec"), sem("m")
        s_mp, s_mev, s_bd = sem("misc_ps"), sem("misc"), sem("bd")
        s_xp, s_xev, s_sps = sem("x_T"), sem("x_T_read"), sem("state_ps")
        s_sd, s_st = sem("sd"), sem("state")
        s_y, s_yev, s_dx, s_gate = sem("y"), sem("y_read"), sem("dx"), sem("gate")
        s_ghi, s_glo, s_sq, s_sum = sem("g_hi"), sem("g_lo"), sem("g_sq"), sem("g_sum")
        s_ss, s_ms, s_ms2, s_rr, s_o, s_out = sem("ss"), sem("ms"), sem("ms2"), sem("rr"), sem("o"), sem("out")

        block = ctx.enter_context(nc.Block())

        pieces = [("in", k, n * (WIN // 2), WIN // 2) for k in range(KD) for n in range(2)]
        pieces += [("out", k, 0, 2 * DM) for k in range(0, KI, 2)]
        stage = [xc[:].rearrange("p k t -> p (k t)"), zs[:].rearrange("p k t -> p (k t)")]

        def piece_at(n, whole_in, whole_out):
            kind, k, c0, w = pieces[n]
            if kind == "in":
                return whole_in[:, k, c0:c0 + w]
            return whole_out[:, k:k + 2, :].rearrange("p k n -> p (k n)")

        def loop(eng, body):
            if first:
                for s in range(NB):
                    body(0, s, False)
            with eng.Fori(b0 + first, b0 + nseq - 1) as b:
                for s in range(NB):
                    body(b, s, False)
            for s in range(NB):
                body(b0 + nseq - 1, s, s == NB - 1)

        @block.sync
        def _(sp):
            sp.dma_start(e[:].rearrange("p a h t -> p (a h t)")[:, 0:K_ID], cst[:, 0:K_ID]).then_inc(s_cst, 16)
            sp.dma_start(small[:], cst[:, K_ID:NCST]).then_inc(s_cst, 16)
            sp.dma_start(prm_sb[:], prm).then_inc(s_prm, 16)

            def load(b, s):
                i = NB * b + s
                sp.wait_ge(s_store[s % 2], 16 * NPAIR * (NB // 2 * b + s // 2))
                sp.dma_start(h_sb[:, s % 2], src[bass.ds((i - NB * b0) * TB, TB), :].rearrange("(t p) d -> p t d", p=P)
                             ).then_inc(s_load[s % 2], 16)

            def load_mod(b):
                sp.wait_ge(s_moda, NB * NPAIR * b)
                sp.dma_start(mod[:], mod_dram[bass.ds(b, 1), 0:2 * DM].rearrange("o (s d) -> o s d", s=2)
                             .broadcast_to([P, 2, DM])).then_inc(s_mod, 16)

            if first:
                load_mod(b0)
            load(b0, 0)
            for n, (kind, k, c0, w) in enumerate(pieces):
                if n >= 2:
                    sp.wait_ge(s_wlo, len(pieces) * layer + n - 1)
                source = in_w[:, k, c0:c0 + w] if kind == "in" else out_w[:, k:k + 2, :].rearrange("p k n -> p (k n)")
                sp.dma_start(stage[n % 2][:, 0:w], source).then_inc(s_stage[n % 2], 16)

            def body(b, s, end):
                i = NB * b + s
                if not end:
                    if s == NB - 1:
                        if first:
                            load_mod(b + 1)
                        load(b + 1, 0)
                    else:
                        load(b, s + 1)
                for j in range(NPAIR):
                    sp.wait_ge(s_out, NPAIR * i + j + 1)
                    sp.dma_start(dst[bass.ds((i - NB * b0) * TB + j * P, P), :], h_sb[:, s % 2, j]
                                 ).then_inc(s_store[s % 2], 16)

            loop(sp, body)
            for k in range(2):
                sp.wait_ge(s_store[k], 16 * NPAIR * NB // 2 * (b0 + nseq))

        @block.tensor
        def _(pe):
            def bank(s, use):
                return (ring_uses * s + use) % 2

            def products(out, pairs):
                n = 3 * len(pairs)
                k = 0
                for (a_hi, a_lo), (b_hi, b_lo) in pairs:
                    for a, c in ((a_lo, b_hi), (a_hi, b_lo), (a_hi, b_hi)):
                        last = nc.tensor.matmul(out, a, c, start=(k == 0), stop=(k == n - 1))
                        k += 1
                return last

            def input_T(b, s, use):
                i = NB * b + s
                pe.wait_ge(s_norm, NPAIR * norm_round(i + 1, 0))
                for half in range(2):
                    out = ring[:, use[half], :].rearrange("p (k t) -> p k t", k=2)
                    for k in range(2):
                        for t in range(NPAIR):
                            d = (2 * half + k) * P
                            last = nc.tensor.transpose(out[:, k, t * P:(t + 1) * P], hn[:, t, d:d + P], ident)
                    last.then_inc(s_ut, 1)

            def project(b, s, n, bk):
                if n == 0:
                    pe.wait_ge(s_ulo, 2 * (NB * b + s + 1))
                for t in range(2):
                    c = (2 * n + t) * P
                    last = products(ring[:, bk, t * TB:(t + 1) * TB],
                                    [((wi_hi[:, k, c:c + P], wi_lo[:, k, c:c + P]), (u_hi[:, k, :], u_lo[:, k, :]))
                                     for k in range(KD)])
                last.then_inc(s_in, 1)

            def front(b, s, j):
                i = NB * b + s
                q = NPAIR * i + j
                if j == 0:
                    pe.wait_ge(s_bc, 2 * (i + 1))
                    pe.wait_ge(s_td, i + 1)
                    pe.wait_ge(s_ms, q)
                else:
                    pe.wait_ge(s_mev, q)
                for k in range(2):
                    c = 2 * j + k
                    nc.tensor.matmul(ps_m[:, 128 + 64 * k:192 + 64 * k], bti[:, c, :],
                                     ct[:, c * CH:(c + 1) * CH], start=True, stop=True)
                nc.tensor.transpose(ps_m[:, 0:64], bt[:, j * P:(j + 1) * P], ident[0:NS, 0:NS])
                nc.tensor.transpose(ps_m[:, 64:128], dt[0:64, j * P:(j + 1) * P], ident[0:NS, 0:NS]
                                    ).then_inc(s_mp, 1)
                if j == 0:
                    pe.wait_ge(s_xc, NX * (i + 1))
                pe.wait_ge(s_e, 2 * q)
                for k in range(KI):
                    last = nc.tensor.transpose(wide[:, 0, k * P:(k + 1) * P], xc[:, k, j * P:(j + 1) * P], ident)
                last.then_inc(s_xp, 1)

            def exponents(b, s, j, odd):
                i = NB * b + s
                q = NPAIR * i + j
                c = 2 * j + odd
                if odd:
                    pe.wait_ge(s_xev, 3 * (q + 1))
                else:
                    pe.wait_ge(s_st, 2 * q)
                pe.wait_ge(s_rhs, 2 * q + odd + 1)
                for n in range(2):
                    last = nc.tensor.matmul(wide[:, 0 if odd else 1, n * 512:(n + 1) * 512], lhs[:, c, :],
                                            rhs[:].rearrange("p h t -> p (h t)")[:, n * 512:(n + 1) * 512],
                                            start=True, stop=True)
                last.then_inc(s_arg, 1)

            def outputs(b, s, j, odd):
                q = NPAIR * (NB * b + s) + j
                pe.wait_ge(s_m, 2 * q + odd + 1)
                if odd:
                    pe.wait_ge(s_st, 2 * q + 1)
                else:
                    pe.wait_ge(s_xev, 3 * (q + 1))
                pe.wait_ge(s_yev, 2 * q + odd)
                for h in range(NH):
                    r = (h % 2) * NS
                    last = nc.tensor.matmul(ps_y[r:r + NS, h // 2, :], xs[:, odd, h * NS:(h + 1) * NS],
                                            e[:, odd, h, :], start=True, stop=True)
                last.then_inc(s_y, 1)

            def states(b, s, j):
                q = NPAIR * (NB * b + s) + j
                pe.wait_ge(s_bd, q + 1)
                pe.wait_ge(s_e, 2 * q + 1)
                for n in range(2):
                    last = nc.tensor.matmul(wide[:, 1, n * 512:(n + 1) * 512], bd[:], xw[:, n * 512:(n + 1) * 512],
                                            start=True, stop=True)
                last.then_inc(s_sps, 1)

            def out_product(b, s, j, bk):
                q = NPAIR * (NB * b + s) + j
                if j == 0:
                    pe.wait_ge(s_mev, q + 2)
                else:
                    pe.wait_ge(s_ms, q)
                pe.wait_ge(s_sum, 3 * (q + 1))
                nc.tensor.matmul(ps_m[:, 0:1], g[:, 0, :], one, start=True, stop=True).then_inc(s_ss, 1)
                pe.wait_ge(s_glo, q + 1)
                products(ring[:, bk, :], [((g_hi[:, k, :], g_lo[:, k, :]), (wo_hi[:, k, :], wo_lo[:, k, :]))
                                          for k in range(KI)]).then_inc(s_o, 1)

            pe.wait_ge(s_cst, 32 * (layer + 1))
            pe.wait_ge(s_wlo, len(pieces) * (layer + 1))
            pe.wait_ge(s_init, 2 * (layer + 1))
            pe.wait_ge(s_cst_copy, 3 * (layer + 1))
            v0 = bank(-1, 8)
            input_T(b0, 0, (v0, 1 - v0))
            pe.wait_ge(s_utev, 2 * NB * b0 + 2)
            project(b0, 0, 0, bank(-1, 11))

            def body(b, s, end):
                i = NB * b + s
                for n in range(1, NG):
                    if n == 2:
                        pe.wait_ge(s_out, NPAIR * i)
                    else:
                        pe.wait_ge(s_inev, NG * i + n - 1 if n > 1 else NG * i + 1)
                    project(b, s, n, bank(s, n - 1))
                    if n == 6:
                        front(b, s, 0)
                        exponents(b, s, 0, 0)
                    if n == 7:
                        exponents(b, s, 0, 1)
                outputs(b, s, 0, 0)
                states(b, s, 0)
                front(b, s, 1)
                outputs(b, s, 0, 1)
                exponents(b, s, 1, 0)
                nb, ns = (b + 1, 0) if s == NB - 1 else (b, s + 1)
                pe.wait_ge(s_inev, NG * (i + 1))
                if not end:
                    input_T(nb, ns, (bank(s, 8), bank(s, 9)))
                    pe.wait_ge(s_utev, 2 * (i + 1) + 1)
                out_product(b, s, 0, bank(s, 10))
                exponents(b, s, 1, 1)
                outputs(b, s, 1, 0)
                states(b, s, 1)
                outputs(b, s, 1, 1)
                if not end:
                    pe.wait_ge(s_utev, 2 * (i + 1) + 2)
                    project(nb, ns, 0, bank(s, 11))
                pe.wait_ge(s_out, NPAIR * i + 1)
                out_product(b, s, 1, bank(s, 12))

            loop(pe, body)

        @block.scalar
        def _(act):
            act.wait_ge(s_prm, 16 * (layer + 1))
            act.wait_ge(s_cst, 32 * (layer + 1))
            nc.scalar.activation(a_neg[:], prm_sb[:, C_ALOG:C_ALOG + 1], ACT.Exp).then_inc(s_aexp, 1)
            for n, (kind, k, c0, w) in enumerate(pieces):
                act.wait_ge(s_stage[n % 2], 16 * (len(pieces) // 2 * layer + n // 2 + 1))
                st = stage[n % 2][:, 0:w]
                if kind == "out":
                    for m in range(2):
                        r = C_RMS + k + m
                        nc.scalar.activation(st[:, m * DM:(m + 1) * DM], st[:, m * DM:(m + 1) * DM], ACT.Identity,
                                             scale=prm_sb[:, r:r + 1]).then_inc(s_wsc, 1)
                    act.wait_ge(s_wsc, KI * layer + k + 2)
                nc.scalar.activation(piece_at(n, wi_hi, wo_hi), st, ACT.Identity).then_inc(s_whi, 1)

            def u_read(b, s):
                i = NB * b + s
                act.wait_ge(s_in, NG * i)
                for half in range(2):
                    act.wait_ge(s_ut, 2 * i + half + 1)
                    act.wait_ge(s_ulo, 2 * i + half)
                    for k in range(2):
                        d = 2 * half + k
                        bk = (ring_uses * (s - 1) + 8 + half) % 2
                        ins = nc.scalar.activation(
                            v[:, k, :], ring[:, bk, k * TB:(k + 1) * TB], ACT.Identity,
                            bias=prm_sb[:, C_LNB + d:C_LNB + d + 1], scale=prm_sb[:, C_LNW + d:C_LNW + d + 1])
                        if k == 1:
                            ins.then_inc(s_utev, 1)
                        else:
                            ins.then_inc(s_v, 1)
                    act.wait_ge(s_utev, 2 * i + half + 1)
                    act.wait_ge(s_v, 2 * i + half + 1)
                    nc.scalar.activation(u_hi[:, 2 * half:2 * half + 2, :], v[:], ACT.Identity).then_inc(s_uhi, 1)

            def conv_in(b, s, n, bk):
                i = NB * b + s
                m = (NX + 1) * i + n
                t0, nt = (0, 1) if n == 0 else (2 * n - 1, 2)
                src_ps = ring[:, bk, (2 - nt) * TB:].rearrange("p (k t) -> p k t", k=nt)
                act.wait_ge(s_acc, m)
                if n >= 1:
                    silu_conv(b, s, n - 1)
                if s == 0:
                    nc.scalar.mul(raw[:, 0:nt, 0:TAPS - 1], small[:, 0:nt * 3].rearrange("p (k t) -> p k t", k=nt),
                                  0.0).then_inc(s_halo, 1)
                else:
                    act.wait_ge(s_halo2, m - (NX + 1) + 1)
                    nc.scalar.copy(raw[:, 0:nt, 0:TAPS - 1], halo[:, t0:t0 + nt, :]).then_inc(s_halo, 1)
                act.wait_ge(s_halo, m + 1)
                nc.scalar.copy(halo[:, t0:t0 + nt, :], src_ps[:, :, TB - TAPS + 1:]).then_inc(s_halo2, 1)
                nc.scalar.copy(raw[:, 0:nt, TAPS - 1:], src_ps).then_inc(s_inev, 1)
                act.wait_ge(s_inev, NG * i + n + 1)
                act.wait_ge(s_bc, 2 * (i + 1) if n >= 1 else 2 * i)
                act.wait_ge(s_xc, NX * i + max(n - 1, 0))
                for k in range(nt):
                    w, bb = C_CW + (t0 + k) * TAPS, C_CB + t0 + k
                    ins = nc.scalar.activation(acc[:, k, :], raw[:, k, 0:TB], ACT.Identity,
                                               bias=prm_sb[:, bb:bb + 1], scale=prm_sb[:, w:w + 1])
                ins.then_inc(s_acc0, 1)

            def silu_conv(b, s, n):
                i = NB * b + s
                act.wait_ge(s_acc, (NX + 1) * i + n + 1)
                if n == 0:
                    view = bti[:].rearrange("n (q c) (a t) -> n q (c a) t", c=2, a=2)[:, :, 0::3, :]
                    nc.scalar.activation(view, acc[0:NS, 0, :].rearrange("n (q c t) -> n q c t", c=2, t=CH),
                                         ACT.Silu)
                    nc.scalar.activation(bt[:], acc[0:NS, 0, :], ACT.Silu).then_inc(s_bc, 1)
                    nc.scalar.activation(ct[:], acc[NS:P, 0, :], ACT.Silu).then_inc(s_bc, 1)
                else:
                    if n == 1:
                        act.wait_ge(s_dx, NPAIR * i)
                    nc.scalar.activation(xc[:, 2 * n - 2:2 * n, :], acc[:], ACT.Silu).then_inc(s_xc, 1)

            def pair_small(b, s, j):
                q = NPAIR * (NB * b + s) + j
                act.wait_ge(s_mp, q + 1)
                act.wait_ge(s_m, 2 * q)
                act.wait_ge(s_bd, q)
                nc.scalar.copy(misc[:].rearrange("p a t -> p (a t)"), ps_m[:, 0:256]).then_inc(s_mev, 1)

            def decays(b, s, j, odd):
                q = NPAIR * (NB * b + s) + j
                act.wait_ge(s_arg, 2 * q + odd + 1)
                nc.scalar.activation(e[:, odd].rearrange("p h t -> p (h t)"), wide[:, 0 if odd else 1, :],
                                     ACT.Exp).then_inc(s_e, 1)

            def split_g(b, s, j):
                q = NPAIR * (NB * b + s) + j
                act.wait_ge(s_gate, q + 1)
                act.wait_ge(s_o, q)
                nc.scalar.activation(g_hi[:], g[:], ACT.Identity).then_inc(s_ghi, 1)
                act.wait_ge(s_glo, q + 1)
                nc.scalar.activation(g[:], g[:], ACT.Square).then_inc(s_sq, 1)

            def body(b, s, end):
                i = NB * b + s
                bk = (ring_uses * (s - 1) + 11) % 2
                act.wait_ge(s_in, NG * i + 1)
                act.wait_ge(s_td, i)
                nc.scalar.activation(dtx[:], ring[:, bk, 0:TB], ACT.Identity,
                                     bias=prm_sb[:, C_DTB:C_DTB + 1]).then_inc(s_xb, 1)
                act.wait_ge(s_xb, i + 1)
                nc.scalar.activation(dty[:], dtx[:], ACT.Abs).then_inc(s_abs, 1)
                act.wait_ge(s_abs, i + 1)
                nc.scalar.activation(dty[:], dty[:], ACT.Exp, scale=-1.0).then_inc(s_exp, 1)
                act.wait_ge(s_exp, i + 1)
                nc.scalar.activation(dty[:], dty[:], ACT.Ln, bias=1.0).then_inc(s_ln, 1)
                conv_in(b, s, 0, bk)
                act.wait_ge(s_dend, i + 1)
                nc.scalar.activation(dty[:], dty[:], ACT.Exp).then_inc(s_wexp, 1)
                for n in range(1, NX + 1):
                    act.wait_ge(s_in, NG * i + n + 1)
                    conv_in(b, s, n, (ring_uses * s + n - 1) % 2)
                for n in range(NX + 1, NG):
                    act.wait_ge(s_in, NG * i + n + 1)
                    if n == NX + 1:
                        act.wait_ge(s_gate, NPAIR * i)
                    m = 2 * (n - NX - 1)
                    nc.scalar.activation(zs[:, m:m + 2, :], ring[:, (ring_uses * s + n - 1) % 2, :]
                                         .rearrange("p (k t) -> p k t", k=2), ACT.Silu).then_inc(s_inev, 1)
                    if n == NX + 1:
                        silu_conv(b, s, NX)
                    if n == NG - 2:
                        pair_small(b, s, 0)
                decays(b, s, 0, 0)
                decays(b, s, 0, 1)
                pair_small(b, s, 1)
                decays(b, s, 1, 0)
                nb, ns = (b + 1, 0) if s == NB - 1 else (b, s + 1)
                if not end:
                    u_read(nb, ns)
                split_g(b, s, 0)
                decays(b, s, 1, 1)
                split_g(b, s, 1)

            u_read(b0, 0)
            loop(act, body)

        @block.vector
        def _(dve):
            dve.wait_ge(s_cst, 32 * (layer + 1))
            stage_c = e[:].rearrange("p a h t -> p (a h t)")
            nc.vector.tensor_copy(rhs[:].rearrange("p h t -> p (h t)"), stage_c[:, K_RHS:K_LHS]).then_inc(s_cst_copy, 1)
            nc.vector.tensor_copy(lhs[:].rearrange("p c t -> p (c t)"), stage_c[:, K_LHS:K_ID]).then_inc(s_cst_copy, 1)
            eye = bti[:].rearrange("n c (a t) -> n (c a) t", a=2)
            for pr in range(2):
                ins = nc.vector.tensor_copy(eye[:, 4 * pr + 1:4 * pr + 3, :],
                                            ident[0:NS, 0:NS].unsqueeze(1).broadcast_to([NS, 2, NS]))
            ins.then_inc(s_cst_copy, 1)
            nc.vector.memset(xs[:], 0.0).then_inc(s_init, 1)
            nc.vector.memset(dec[:], 0.0).then_inc(s_init, 1)
            dve.wait_ge(s_aexp, layer + 1)
            nc.vector.tensor_scalar_mul(a_neg[:], a_neg[:], -1.0).then_inc(s_aneg, 1)
            for n, (kind, k, c0, w) in enumerate(pieces):
                dve.wait_ge(s_whi, len(pieces) * layer + n + 1)
                nc.vector.tensor_tensor(piece_at(n, wi_lo, wo_lo), stage[n % 2][:, 0:w],
                                        piece_at(n, wi_hi, wo_hi).bitcast(F32), ALU.subtract).then_inc(s_wlo, 1)

            def row_stats(b, s, rnd):
                i = NB * b + s
                m = NPAIR * norm_round(i, rnd)
                if rnd == 0:
                    dve.wait_ge(s_load[s % 2], 16 * (NB // 2 * b + s // 2 + 1))
                else:
                    dve.wait_ge(s_moda, NPAIR * (i + 1))
                dve.wait_ge(s_mv, m)
                for t in range(NPAIR):
                    nc.vector.bn_stats(stats[:, t, :], h_sb[:, s % 2, t, :]).then_inc(s_bn, 1)
                dve.wait_ge(s_norm, m)
                dve.wait_ge(s_bn, m + NPAIR)
                nc.vector.memset(spare[:], 0.0)
                for t in range(NPAIR):
                    nc.vector.bn_aggr(mv[:, t, :], stats[:, t, :]).then_inc(s_mv, 1)

            def normalise(b, s, rnd):
                i = NB * b + s
                m = norm_round(i, rnd)
                dve.wait_ge(s_rstd, m + 1)
                if rnd == rounds - 1:
                    dve.wait_ge(s_ut, 2 * i)
                for t in range(NPAIR):
                    out = hn[:, t, :] if rnd == rounds - 1 else h_sb[:, s % 2, t, :]
                    nc.vector.tensor_scalar(out, h_sb[:, s % 2, t, :], mv[:, t, 0:1], rstd[:, t:t + 1],
                                            ALU.subtract, ALU.mult).then_inc(s_norm, 1)

            def split_u(b, s):
                i = NB * b + s
                for half in range(2):
                    dve.wait_ge(s_uhi, 2 * i + half + 1)
                    k = slice(2 * half, 2 * half + 2)
                    nc.vector.tensor_tensor(u_lo[:, k, :], v[:], u_hi[:, k, :].bitcast(F32),
                                            ALU.subtract).then_inc(s_ulo, 1)

            def steps(b, s):
                i = NB * b + s
                dve.wait_ge(s_ln, i + 1)
                nc.vector.scalar_tensor_tensor(out=dt[:], in0=dtx[:], scalar=0.0, in1=dty[:], op0=ALU.max,
                                               op1=ALU.add).then_inc(s_dt, 1)
                dve.wait_ge(s_dt, i + 1)
                nc.vector.tensor_scalar(dtx[:], dt[:], a_neg[:], None, ALU.mult).then_inc(s_a, 1)
                dve.wait_ge(s_a, i + 1)
                dve.wait_ge(s_rhs, 2 * NPAIR * i)
                nc.vector.tensor_tensor_scan(cum[:], const(K_SCAN, TB), dtx[:], 0.0, ALU.mult, ALU.add
                                             ).then_inc(s_cum, 1)
                dve.wait_ge(s_cum, i + 1)
                nc.vector.tensor_copy(chi[:], cum[:]).then_inc(s_chi, 1)
                c4 = cum[:].rearrange("p (c t) -> p c t", t=CH)
                nc.vector.tensor_tensor(dty[:].rearrange("p (c t) -> p c t", t=CH),
                                        c4[:, :, CH - 1:CH].broadcast_to([P, TB // CH, CH]), c4,
                                        ALU.subtract).then_inc(s_dend, 1)
                dve.wait_ge(s_chi, i + 1)
                nc.vector.tensor_scalar(dtx[:], chi[:].bitcast(F32), const(K_LOW, 1), None, ALU.mult
                                        ).then_inc(s_vr, 1)
                dve.wait_ge(s_vr, 2 * i + 1)
                nc.vector.tensor_tensor(cum[:], cum[:], dtx[:], ALU.subtract).then_inc(s_vr, 1)
                dve.wait_ge(s_vr, 2 * i + 2)
                dve.wait_ge(s_dend, i + 1)
                lv = lhs[32:64].rearrange("p c (a t) -> p (c a) t", a=2)
                cv = cum[32:64, :].rearrange("p (c t) -> p c t", t=CH)
                for pr in range(2):
                    nc.vector.tensor_scalar(lv[:, 4 * pr:4 * pr + 4:3, :], cv[:, 2 * pr:2 * pr + 2, :], -1.0, None,
                                            ALU.mult).then_inc(s_lhs, 1)

            def step_weights(b, s):
                i = NB * b + s
                dve.wait_ge(s_wexp, i + 1)
                nc.vector.tensor_tensor(dt[32:64, :], dt[32:64, :], dty[32:64, :], ALU.mult).then_inc(s_td, 1)

            def taps(b, s, n):
                i = NB * b + s
                m = (NX + 1) * i + n
                t0, nt = (0, 1) if n == 0 else (2 * n - 1, 2)
                dve.wait_ge(s_acc0, m + 1)
                for tap in range(1, TAPS):
                    for k in range(nt):
                        w = C_CW + (t0 + k) * TAPS + tap
                        ins = nc.vector.scalar_tensor_tensor(
                            out=acc[:, k, :], in0=raw[:, k, tap:tap + TB], scalar=prm_sb[:, w:w + 1],
                            in1=acc[:, k, :], op0=ALU.mult, op1=ALU.add)
                        if tap < TAPS - 1:
                            ins.then_inc(s_tap, 1)
                        elif k == nt - 1:
                            ins.then_inc(s_acc, 1)
                    if tap < TAPS - 1:
                        base = 18 * i + (0 if n == 0 else 2 + 4 * (n - 1))
                        dve.wait_ge(s_tap, base + tap * nt)

            def x_read(b, s, j):
                q = NPAIR * (NB * b + s) + j
                dve.wait_ge(s_xp, q + 1)
                dve.wait_ge(s_mev, q + 1)

                def scaled(out, rows, col):
                    pt = wide[rows, 0, :].rearrange("p (h n) -> p h n", n=NS)
                    nc.vector.tensor_tensor(out.rearrange("p (h n) -> p h n", n=NS), pt,
                                            misc[rows, 1, col:col + NH].unsqueeze(2)
                                            .broadcast_to([out.shape[0], NH, NS]), ALU.mult).then_inc(s_xev, 1)

                scaled(xs[0:CH, 0, :], slice(0, CH), 0)
                scaled(xw[:], slice(0, P), 32)
                dve.wait_ge(s_y, 2 * q)
                scaled(xs[CH:P, 1, :], slice(CH, P), 0)

            def matrices(b, s, j, odd):
                q = NPAIR * (NB * b + s) + j
                n = 2 * q + odd
                dve.wait_ge(s_e, n + 1)
                dve.wait_ge(s_sd, 2 * q)
                rows = slice(0, CH) if odd else slice(CH, P)
                nc.vector.tensor_copy(dec[rows, odd, :], e[rows, odd, :, CH - 1]).then_inc(s_dec, 1)
                dve.wait_ge(s_dec, n + 1)
                dve.wait_ge(s_mev, q + 1)
                nc.vector.tensor_tensor(e[:, odd], e[:, odd],
                                        misc[:, 2 + odd, :].unsqueeze(1).broadcast_to([P, NH, CH]),
                                        ALU.mult).then_inc(s_m, 1)

            def new_state(b, s, j, odd):
                q = NPAIR * (NB * b + s) + j
                if odd and j == NPAIR - 1 and s == NB - 1:
                    dve.wait_ge(s_st, 2 * q + 1)
                    dve.wait_ge(s_y, 2 * q + 1)
                    dve.wait_ge(s_sd, 2 * q + 1)
                    nc.vector.memset(xs[CH:P, 0, :], 0.0).then_inc(s_st, 1)
                    return
                dve.wait_ge(s_sd, 2 * q + odd + 1)
                dve.wait_ge(s_sps, q + 1)
                if odd:
                    dve.wait_ge(s_y, 2 * q + 1)
                    nc.vector.tensor_tensor(xs[CH:P, 0, :], sd[0:CH, :], wide[CH:P, 1, :], ALU.add).then_inc(s_st, 1)
                else:
                    nc.vector.tensor_tensor(xs[0:CH, 1, :], sd[CH:P, :], wide[0:CH, 1, :], ALU.add).then_inc(s_st, 1)

            def y_read(b, s, j, odd):
                q = NPAIR * (NB * b + s) + j
                dve.wait_ge(s_y, 2 * q + odd + 1)
                dve.wait_ge(s_dx, q + 1)
                gv = g[:, :, odd * CH:(odd + 1) * CH]
                nc.vector.tensor_tensor(gv, gv, ps_y[:], ALU.add).then_inc(s_yev, 1)

            def split_g(b, s, j):
                q = NPAIR * (NB * b + s) + j
                dve.wait_ge(s_ghi, q + 1)
                nc.vector.tensor_tensor(g_lo[:], g[:], g_hi[:].bitcast(F32), ALU.subtract).then_inc(s_glo, 1)

            def finish(b, s, j):
                q = NPAIR * (NB * b + s) + j
                dve.wait_ge(s_ss, q + 1)
                dve.wait_ge(s_rr, q)
                nc.vector.tensor_scalar(ms[:], ps_m[:, 0:1], 1.0 / DI, EPS, ALU.mult, ALU.add).then_inc(s_ms, 1)
                dve.wait_ge(s_o, q + 1)
                dve.wait_ge(s_rr, q + 1)
                bk = (ring_uses * s + (10 if j == 0 else 12)) % 2
                nc.vector.scalar_tensor_tensor(out=h_sb[:, s % 2, j, :], in0=ring[:, bk, :], scalar=rr[:],
                                               in1=h_sb[:, s % 2, j, :], op0=ALU.mult, op1=ALU.add
                                               ).then_inc(s_out, 1)

            def body(b, s, end):
                nb, ns = (b + 1, 0) if s == NB - 1 else (b, s + 1)
                steps(b, s)
                taps(b, s, 0)
                step_weights(b, s)
                taps(b, s, 1)
                if not end:
                    row_stats(nb, ns, 0)
                taps(b, s, 2)
                if not end:
                    normalise(nb, ns, 0)
                taps(b, s, 3)
                taps(b, s, 4)
                if first and not end:
                    row_stats(nb, ns, 1)
                x_read(b, s, 0)
                if first and not end:
                    normalise(nb, ns, 1)
                matrices(b, s, 0, 0)
                matrices(b, s, 0, 1)
                y_read(b, s, 0, 0)
                new_state(b, s, 0, 0)
                new_state(b, s, 0, 1)
                y_read(b, s, 0, 1)
                x_read(b, s, 1)
                matrices(b, s, 1, 0)
                if not end:
                    split_u(nb, ns)
                split_g(b, s, 0)
                matrices(b, s, 1, 1)
                finish(b, s, 0)
                y_read(b, s, 1, 0)
                new_state(b, s, 1, 0)
                new_state(b, s, 1, 1)
                y_read(b, s, 1, 1)
                split_g(b, s, 1)
                finish(b, s, 1)

            for rnd in range(rounds):
                row_stats(b0, 0, rnd)
                normalise(b0, 0, rnd)
            split_u(b0, 0)
            loop(dve, body)

        @block.gpsimd
        def _(pool):
            def inv_std(b, s, rnd):
                m = norm_round(NB * b + s, rnd)
                pool.wait_ge(s_mv, NPAIR * (m + 1))
                pool.wait_ge(s_norm, NPAIR * m)
                nc.gpsimd.tensor_tensor(rstd[:], mv[:, :, 1], const(K_EPS, 2), ALU.add).then_inc(s_var, 1)
                pool.wait_ge(s_var, m + 1)
                nc.gpsimd.tensor_tensor(rstd[:], rstd[:], const(K_HALF, 2), ALU.pow).then_inc(s_rstd, 1)

            def modulate(b, s):
                i = NB * b + s
                pool.wait_ge(s_mod, 16 * (b + 1))
                pool.wait_ge(s_norm, NPAIR * (2 * i + 1))
                for t in range(NPAIR):
                    h = h_sb[:, s % 2, t, :]
                    nc.gpsimd.tensor_tensor(h, h, mod[:, 1, :], ALU.mult).then_inc(s_modm, 1)
                    pool.wait_ge(s_modm, NPAIR * i + t + 1)
                    nc.gpsimd.tensor_tensor(h, h, mod[:, 0, :], ALU.add).then_inc(s_moda, 1)

            def moving(b, s, c):
                n = 2 * NPAIR * (NB * b + s) + c
                pool.wait_ge(s_arg, n)
                if c == 0:
                    pool.wait_ge(s_lhs, 2 * (NB * b + s + 1))
                nc.gpsimd.tensor_tensor(rhs[0:32], cum[0:32, c * CH:(c + 1) * CH].unsqueeze(1)
                                        .broadcast_to([32, NH, CH]),
                                        const(K_DELTA, NH)[0:32].unsqueeze(2).broadcast_to([32, NH, CH]),
                                        ALU.mult).then_inc(s_rhs, 1)

            def diagonal(b, s, j):
                q = NPAIR * (NB * b + s) + j
                pool.wait_ge(s_mev, q + 1)
                pool.wait_ge(s_sps, q)
                nc.gpsimd.tensor_tensor(bd[:].rearrange("p (c n) -> p c n", c=2),
                                        misc[:, 0, :].unsqueeze(1).broadcast_to([P, 2, NS]),
                                        const(K_BLK, 2).unsqueeze(2).broadcast_to([P, 2, NS]),
                                        ALU.mult).then_inc(s_bd, 1)

            def skip_term(b, s, j):
                i = NB * b + s
                q = NPAIR * i + j
                pool.wait_ge(s_xc, NX * (i + 1))
                pool.wait_ge(s_ss, q)
                nc.gpsimd.tensor_tensor(g[:], xc[:, :, j * P:(j + 1) * P],
                                        prm_sb[:, C_D:C_D + KI].unsqueeze(2).broadcast_to([P, KI, P]),
                                        ALU.mult).then_inc(s_dx, 1)

            def decay_state(b, s, j, odd):
                q = NPAIR * (NB * b + s) + j
                pool.wait_ge(s_dec, 2 * q + odd + 1)
                pool.wait_ge(s_st, 2 * q + odd)
                nc.gpsimd.tensor_tensor(sd[:].rearrange("p (h n) -> p h n", n=NS),
                                        xs[:, odd, :].rearrange("p (h n) -> p h n", n=NS),
                                        dec[:, odd, :].unsqueeze(2).broadcast_to([P, NH, NS]),
                                        ALU.mult).then_inc(s_sd, 1)

            def gate(b, s, j):
                q = NPAIR * (NB * b + s) + j
                pool.wait_ge(s_yev, 2 * q + 2)
                if j == 0:
                    pool.wait_ge(s_inev, NG * (NB * b + s + 1))
                nc.gpsimd.tensor_tensor(g[:], g[:], zs[:, :, j * P:(j + 1) * P], ALU.mult).then_inc(s_gate, 1)

            def squares(b, s, j):
                q = NPAIR * (NB * b + s) + j
                pool.wait_ge(s_sq, q + 1)
                for n, w in enumerate((4, 2, 1)):
                    if n:
                        pool.wait_ge(s_sum, 3 * q + n)
                    nc.gpsimd.tensor_tensor(g[:, 0:w], g[:, 0:w], g[:, w:2 * w], ALU.add).then_inc(s_sum, 1)

            def inv_rms(b, s, j):
                q = NPAIR * (NB * b + s) + j
                pool.wait_ge(s_ms, q + 1)
                pool.wait_ge(s_out, q)
                nc.gpsimd.tensor_tensor(rr[:], ms[:], const(K_HALF, 1), ALU.pow).then_inc(s_rr, 1)

            def body(b, s, end):
                nb, ns = (b + 1, 0) if s == NB - 1 else (b, s + 1)
                moving(b, s, 0)
                if not end:
                    inv_std(nb, ns, 0)
                    if first:
                        modulate(nb, ns)
                        inv_std(nb, ns, 1)
                skip_term(b, s, 0)
                diagonal(b, s, 0)
                moving(b, s, 1)
                decay_state(b, s, 0, 0)
                moving(b, s, 2)
                decay_state(b, s, 0, 1)
                diagonal(b, s, 1)
                gate(b, s, 0)
                moving(b, s, 3)
                squares(b, s, 0)
                inv_rms(b, s, 0)
                skip_term(b, s, 1)
                decay_state(b, s, 1, 0)
                decay_state(b, s, 1, 1)
                gate(b, s, 1)
                squares(b, s, 1)
                inv_rms(b, s, 1)

            pool.wait_ge(s_cst, 32 * (layer + 1))
            pool.wait_ge(s_prm, 16 * (layer + 1))
            pool.wait_ge(s_init, 2 * (layer + 1))
            for rnd in range(rounds):
                inv_std(b0, 0, rnd)
                if first and rnd == 0:
                    modulate(b0, 0)
            loop(pool, body)


def channel_mix(nc, sems, x_in, h_in, out, w3, prm, cst, mod_dram, mod_cols, nseq):
    T = 512
    NT = T // P
    halves = 2
    with ExitStack() as ctx:
        def sb(name, shape, dt=F32):
            return ctx.enter_context(nc.sbuf_tensor("f_" + name, shape, dt))

        def psum(name):
            return ctx.enter_context(nc.psum_tensor("f_" + name, [P, 2, 512], F32))

        def sem(name):
            return sems("f_" + name)

        w_hi = [sb(f"w_hi{n}", [P, KD, DM], F32R) for n in range(3)]
        w_lo = [sb(f"w_lo{n}", [P, KD, DM], F32R) for n in range(3)]
        prm_sb = sb("prm", [P, 2 * KD])
        small = sb("small", [P, NCST - K_ID])
        x = sb("x", [P, 2, NT, DM])
        h2 = sb("h2", [P, 2, NT, DM])
        hn = sb("hn", [P, NT, DM])
        ht = sb("ht", [P, KD, T + 1])
        diff = sb("diff", [P, T])
        mixed = sb("mixed", [P, 2, T])
        m_hi = [sb("r_hi", [P, KD, T], F32R), sb("k_hi", [P, KD, T], F32R)]
        m_lo = [sb("r_lo", [P, KD, T], F32R), sb("k_lo", [P, KD, T], F32R)]
        kr, ka = sb("kr", [P, T]), sb("ka", [P, T])
        ka_hi, ka_lo = sb("ka_hi", [P, KD, T], F32R), sb("ka_lo", [P, KD, T], F32R)
        rs = sb("rs", [P, NT, DM])
        gates = sb("gates", [P, 2, DM])
        spare = sb("spare", [P, 1])
        shift = sb("shift", [P, 2, KD])
        stats, mv, rstd = sb("stats", [P, NT, 6]), sb("mv", [P, NT, 2]), sb("rstd", [P, NT])
        ps_k, ps_r, ps_v, ps_t = psum("ps_k"), psum("ps_r"), psum("ps_v"), psum("ps_t")

        s_cst, s_stage, s_whi, s_wlo = sem("cst"), [sem("stage0"), sem("stage1")], sem("w_hi"), sem("w_lo")
        s_load, s_store = [sem("load0"), sem("load1")], [sem("store0"), sem("store1")]
        s_gal, s_gbl, s_shift = sem("ga_loaded"), sem("gb_loaded"), sem("shift")
        s_ga, s_x2 = sem("ga"), sem("x2")
        s_bn, s_mv, s_var, s_rstd, s_norm = sem("bn"), sem("mv"), sem("var"), sem("rstd"), sem("norm")
        s_t, s_ht, s_edge, s_diff, s_mix, s_mhi, s_mlo = (
            sem("t"), sem("ht"), sem("edge"), sem("diff"), sem("mix"), sem("m_hi"), sem("m_lo"))
        s_k, s_kr, s_ka, s_kahi, s_kalo = sem("k"), sem("kr"), sem("ka"), sem("ka_hi"), sem("ka_lo")
        s_r, s_rs, s_v, s_o, s_gb, s_y = sem("r"), sem("rs"), sem("v"), sem("o"), sem("gb"), sem("y")
        block = ctx.enter_context(nc.Block())

        ident = small[:, 0:P]
        stage = [hn[:].rearrange("p t d -> p (t d)"), rs[:].rearrange("p t d -> p (t d)")]

        def loop(eng, body):
            for s in range(halves):
                body(0, s, False)
            with eng.Fori(1, nseq - 1) as b:
                for s in range(halves):
                    body(b, s, False)
            for s in range(halves):
                body(nseq - 1, s, s == halves - 1)

        def after(b, s):
            return (b + 1, 0) if s == halves - 1 else (b, s + 1)

        @block.sync
        def _(sp):
            sp.dma_start(small[:], cst[:, K_ID:NCST]).then_inc(s_cst, 16)
            sp.dma_start(prm_sb[:], prm).then_inc(s_cst, 16)

            def load(b, s):
                i = halves * b + s
                sp.wait_ge(s_store[s], 16 * NT * b)
                for src, to in ((x_in, x), (h_in, h2)):
                    sp.dma_start(to[:, s], src[bass.ds(i * T, T), :].rearrange("(t p) d -> p t d", p=P)
                                 ).then_inc(s_load[s], 16)

            for n in range(3):
                if n == 2:
                    sp.wait_ge(s_wlo, 1)
                sp.dma_start(stage[n % 2], w3[n].rearrange("p k n -> p (k n)")).then_inc(s_stage[n % 2], 16)

            def load_shift(b):
                sp.wait_ge(s_ht, halves * KD * b)
                sp.dma_start(shift[:], mod_cols[bass.ds(b, 1)].rearrange("o p (s k) -> (o p) s k", s=2)
                             ).then_inc(s_shift, 16)

            def load_ga(b):
                sp.wait_ge(s_ga, halves * NT * b)
                sp.dma_start(gates[:, 0, :], mod_dram[bass.ds(b, 1), 2 * DM:3 * DM].broadcast_to([P, DM])
                             ).then_inc(s_gal, 16)

            def load_gb(b):
                sp.wait_ge(s_gb, halves * NT * b)
                sp.dma_start(gates[:, 1, :], mod_dram[bass.ds(b, 1), 5 * DM:6 * DM].broadcast_to([P, DM])
                             ).then_inc(s_gbl, 16)

            load_shift(0)
            load_ga(0)
            load_gb(0)
            load(0, 0)

            def body(b, s, end):
                i = halves * b + s
                nb, ns = after(b, s)
                if s == 0:
                    load(nb, ns)
                for t in range(NT):
                    sp.wait_ge(s_y, NT * i + t + 1)
                    sp.dma_start(out[bass.ds(i * T + t * P, P), :], x[:, s, t, :]).then_inc(s_store[s], 16)
                if isinstance(b, int) and b == nseq - 1:
                    return
                if s == 0:
                    load(b + 1, 0)
                    load_shift(b + 1)
                    load_ga(b + 1)
                else:
                    load_gb(b + 1)

            loop(sp, body)
            for k in range(2):
                sp.wait_ge(s_store[k], 16 * NT * nseq)

        @block.tensor
        def _(pe):
            def products(out_ps, parts):
                n, k = 3 * len(parts), 0
                for (a_hi, a_lo), (b_hi, b_lo) in parts:
                    for a, c in ((a_lo, b_hi), (a_hi, b_lo), (a_hi, b_hi)):
                        last = nc.tensor.matmul(out_ps, a, c, start=(k == 0), stop=(k == n - 1))
                        k += 1
                return last

            def bank_free(sem_read, i, m):
                pe.wait_ge(sem_read, 4 * i + m - 1 if m >= 2 else 4 * i)

            def turn(b, s):
                i = halves * b + s
                pe.wait_ge(s_norm, NT * (i + 1))
                for d in range(KD):
                    bank_free(s_ht, i, d)
                    for t in range(NT):
                        last = nc.tensor.transpose(ps_t[:, d % 2, t * P:(t + 1) * P], hn[:, t, d * P:(d + 1) * P],
                                                   ident)
                    last.then_inc(s_t, 1)

            pe.wait_ge(s_cst, 32)
            pe.wait_ge(s_wlo, 3)
            turn(0, 0)

            def body(b, s, end):
                i = halves * b + s
                pe.wait_ge(s_mlo, 2 * KD * (i + 1))
                for m in range(KD):
                    bank_free(s_kr, i, m)
                    c = slice(m * P, (m + 1) * P)
                    products(ps_k[:, m % 2, :], [((w_hi[1][:, k, c], w_lo[1][:, k, c]),
                                                  (m_hi[1][:, k, :], m_lo[1][:, k, :])) for k in range(KD)]
                             ).then_inc(s_k, 1)
                for t in range(NT):
                    bank_free(s_rs, i, t)
                    c = slice(t * P, (t + 1) * P)
                    products(ps_r[:, t % 2, :], [((m_hi[0][:, k, c], m_lo[0][:, k, c]),
                                                  (w_hi[0][:, k, :], w_lo[0][:, k, :])) for k in range(KD)]
                             ).then_inc(s_r, 1)
                if not end:
                    turn(*after(b, s))
                pe.wait_ge(s_kalo, KD * (i + 1))
                for t in range(NT):
                    bank_free(s_o, i, t)
                    c = slice(t * P, (t + 1) * P)
                    products(ps_v[:, t % 2, :], [((ka_hi[:, k, c], ka_lo[:, k, c]),
                                                  (w_hi[2][:, k, :], w_lo[2][:, k, :])) for k in range(KD)]
                             ).then_inc(s_v, 1)

            loop(pe, body)

        @block.scalar
        def _(act):
            for n in range(3):
                act.wait_ge(s_stage[n % 2], 16 * (n // 2 + 1))
                nc.scalar.activation(w_hi[n][:].rearrange("p k n -> p (k n)"), stage[n % 2], ACT.Identity
                                     ).then_inc(s_whi, 1)

            def affine(b, s):
                i = halves * b + s
                act.wait_ge(s_shift, 16 * (b + 1))
                act.wait_ge(s_mix, 2 * KD * i)
                if s == 0:
                    nc.scalar.mul(ht[:, :, 0:1], ident[:, 0:KD].unsqueeze(2), 0.0).then_inc(s_edge, 1)
                else:
                    act.wait_ge(s_ht, KD * i)
                    nc.scalar.copy(ht[:, :, 0:1], ht[:, :, T:T + 1]).then_inc(s_edge, 1)
                act.wait_ge(s_edge, i + 1)
                for d in range(KD):
                    act.wait_ge(s_t, KD * i + d + 1)
                    nc.scalar.activation(ht[:, d, 1:], ps_t[:, d % 2, :], ACT.Identity,
                                         bias=shift[:, 0, d:d + 1], scale=shift[:, 1, d:d + 1]).then_inc(s_ht, 1)
                    if d:
                        high(b, s, d - 1)
                high(b, s, KD - 1)

            def high(b, s, d):
                i = halves * b + s
                for m in range(2):
                    n = 2 * (KD * i + d) + m
                    act.wait_ge(s_mix, n + 1)
                    nc.scalar.activation(m_hi[m][:, d, :], mixed[:, m, :], ACT.Identity).then_inc(s_mhi, 1)

            affine(0, 0)

            def body(b, s, end):
                i = halves * b + s
                for m in range(KD):
                    act.wait_ge(s_k, KD * i + m + 1)
                    act.wait_ge(s_ka, KD * i + m)
                    nc.scalar.activation(kr[:], ps_k[:, m % 2, :], ACT.Relu).then_inc(s_kr, 1)
                    act.wait_ge(s_ka, KD * i + m + 1)
                    if m == 0:
                        act.wait_ge(s_v, NT * i)
                    nc.scalar.activation(ka_hi[:, m, :], ka[:], ACT.Identity).then_inc(s_kahi, 1)
                for t in range(NT):
                    act.wait_ge(s_r, NT * i + t + 1)
                    if t == 0:
                        act.wait_ge(s_y, NT * i)
                    nc.scalar.activation(rs[:, t, :], ps_r[:, t % 2, :], ACT.Sigmoid).then_inc(s_rs, 1)
                if not end:
                    affine(*after(b, s))

            loop(act, body)

        @block.vector
        def _(dve):
            dve.wait_ge(s_cst, 32)
            for n in range(3):
                dve.wait_ge(s_whi, n + 1)
                nc.vector.tensor_tensor(w_lo[n][:].rearrange("p k n -> p (k n)"), stage[n % 2],
                                        w_hi[n][:].rearrange("p k n -> p (k n)").bitcast(F32), ALU.subtract
                                        ).then_inc(s_wlo, 1)

            def norm(b, s):
                i = halves * b + s
                dve.wait_ge(s_mv, NT * i)
                dve.wait_ge(s_norm, NT * i)
                for t in range(NT):
                    dve.wait_ge(s_x2, NT * i + t + 1)
                    nc.vector.bn_stats(stats[:, t, :], x[:, s, t, :]).then_inc(s_bn, 1)
                dve.wait_ge(s_bn, NT * (i + 1))
                nc.vector.memset(spare[:], 0.0)
                for t in range(NT):
                    nc.vector.bn_aggr(mv[:, t, :], stats[:, t, :]).then_inc(s_mv, 1)
                dve.wait_ge(s_rstd, i + 1)
                dve.wait_ge(s_t, KD * i)
                for t in range(NT):
                    nc.vector.tensor_scalar(hn[:, t, :], x[:, s, t, :], mv[:, t, 0:1], rstd[:, t:t + 1],
                                            ALU.subtract, ALU.mult).then_inc(s_norm, 1)

            def mix(b, s, d):
                i = halves * b + s
                n = KD * i + d
                dve.wait_ge(s_diff, n + 1)
                dve.wait_ge(s_ht, n + 1)
                dve.wait_ge(s_mlo, 2 * n)
                for m in range(2):
                    nc.vector.scalar_tensor_tensor(out=mixed[:, m, :], in0=diff[:], scalar=prm_sb[:, m * KD + d:m * KD + d + 1],
                                                   in1=ht[:, d, 0:T], op0=ALU.mult, op1=ALU.add).then_inc(s_mix, 1)
                for m in range(2):
                    dve.wait_ge(s_mhi, 2 * n + m + 1)
                    nc.vector.tensor_tensor(m_lo[m][:, d, :], mixed[:, m, :], m_hi[m][:, d, :].bitcast(F32),
                                            ALU.subtract).then_inc(s_mlo, 1)

            norm(0, 0)
            for d in range(KD):
                mix(0, 0, d)

            def body(b, s, end):
                i = halves * b + s
                for m in range(KD):
                    dve.wait_ge(s_kahi, KD * i + m + 1)
                    nc.vector.tensor_tensor(ka_lo[:, m, :], ka[:], ka_hi[:, m, :].bitcast(F32), ALU.subtract
                                            ).then_inc(s_kalo, 1)
                if not end:
                    norm(*after(b, s))
                for t in range(NT):
                    if not end:
                        mix(*after(b, s), t)
                    dve.wait_ge(s_v, NT * i + t + 1)
                    dve.wait_ge(s_rs, NT * i + t + 1)
                    nc.vector.tensor_tensor(rs[:, t, :], rs[:, t, :], ps_v[:, t % 2, :], ALU.mult).then_inc(s_o, 1)

            loop(dve, body)

        @block.gpsimd
        def _(pool):
            pool.wait_ge(s_cst, 32)

            def residual(b, s):
                i = halves * b + s
                pool.wait_ge(s_gal, 16 * (b + 1))
                pool.wait_ge(s_load[s], 32 * (b + 1))
                for t in range(NT):
                    nc.gpsimd.tensor_tensor(h2[:, s, t, :], h2[:, s, t, :], gates[:, 0, :], ALU.mult
                                            ).then_inc(s_ga, 1)
                    pool.wait_ge(s_ga, NT * i + t + 1)
                    nc.gpsimd.tensor_tensor(x[:, s, t, :], x[:, s, t, :], h2[:, s, t, :], ALU.add
                                            ).then_inc(s_x2, 1)

            def inv_std(b, s):
                i = halves * b + s
                pool.wait_ge(s_mv, NT * (i + 1))
                pool.wait_ge(s_norm, NT * i)
                eps = small[:, K_EPS - K_ID:K_EPS - K_ID + 1].broadcast_to([P, NT])
                half = small[:, K_HALF - K_ID:K_HALF - K_ID + 1].broadcast_to([P, NT])
                nc.gpsimd.tensor_tensor(rstd[:], mv[:, :, 1], eps, ALU.add).then_inc(s_var, 1)
                pool.wait_ge(s_var, i + 1)
                nc.gpsimd.tensor_tensor(rstd[:], rstd[:], half, ALU.pow).then_inc(s_rstd, 1)

            def difference(b, s, d):
                n = KD * (halves * b + s) + d
                pool.wait_ge(s_ht, n + 1)
                pool.wait_ge(s_mix, 2 * n)
                nc.gpsimd.tensor_tensor(diff[:], ht[:, d, 1:], ht[:, d, 0:T], ALU.subtract).then_inc(s_diff, 1)

            residual(0, 0)
            inv_std(0, 0)
            for d in range(KD):
                difference(0, 0, d)

            def body(b, s, end):
                i = halves * b + s
                if not end:
                    residual(*after(b, s))
                for m in range(KD):
                    pool.wait_ge(s_kr, KD * i + m + 1)
                    pool.wait_ge(s_kalo, KD * i + m)
                    nc.gpsimd.tensor_tensor(ka[:], kr[:], kr[:], ALU.mult).then_inc(s_ka, 1)
                if not end:
                    inv_std(*after(b, s))
                pool.wait_ge(s_gbl, 16 * (b + 1))
                for t in range(NT):
                    if not end:
                        difference(*after(b, s), t)
                    pool.wait_ge(s_o, NT * i + t + 1)
                    nc.gpsimd.tensor_tensor(rs[:, t, :], rs[:, t, :], gates[:, 1, :], ALU.mult).then_inc(s_gb, 1)
                    pool.wait_ge(s_gb, NT * i + t + 1)
                    nc.gpsimd.tensor_tensor(x[:, s, t, :], x[:, s, t, :], rs[:, t, :], ALU.add).then_inc(s_y, 1)

            loop(pool, body)


def build(nc, x, in_w, out_w, prm, w3, fprm, cT, wmod, cst, out, nseq):
    rows = x.shape[0]
    mod_dram = nc.dram_tensor("mod_scratch", [nseq, 6 * DM], F32, kind="Internal").ap()
    h1 = nc.dram_tensor("h1_scratch", [rows, DM], F32, kind="Internal").ap()
    h2 = nc.dram_tensor("h2_scratch", [rows, DM], F32, kind="Internal").ap()
    mod_cols = nc.dram_tensor("mod_cols_scratch", [nseq, P, 2 * KD], F32, kind="Internal").ap()
    with ExitStack() as ctx:
        known = {}

        def sems(name):
            if name not in known:
                known[name] = ctx.enter_context(nc.semaphore(name))
            return known[name]

        modulation(nc, sems, cT, wmod, cst, mod_dram, mod_cols, nseq)
        mamba_layer(nc, sems, 0, x, h1, in_w[0], out_w[0], prm[0], cst, mod_dram, nseq)
        mamba_layer(nc, sems, 1, h1, h2, in_w[1], out_w[1], prm[1], cst, mod_dram, nseq)
        channel_mix(nc, sems, x, h2, out, w3, fprm, cst, mod_dram, mod_cols, nseq)


def layout(inputs):
    g = {k: np.ascontiguousarray(v) for k, v in inputs.items()}

    def tiles(w):
        return w.reshape(w.shape[0] // P, P, w.shape[1]).transpose(1, 0, 2)

    def cols(vec):
        return vec.reshape(-1, P).T

    in_w, out_w, prm = [], [], []
    for n in range(NL):
        w = g["L0_attn_in_proj_w"][n]
        z, xx, bc, dt = w[:DI], w[DI:2 * DI], w[2 * DI:2 * DI + 2 * NS], w[2 * DI + 2 * NS:]
        in_w.append(tiles(np.concatenate([dt] * (P // NH) + [bc, xx, z]).T))
        out_w.append(tiles(g["L0_attn_out_proj_w"][n].T))
        cw, cb = g["L0_attn_conv_w"][n], g["L0_attn_conv_b"][n]
        cw = np.concatenate([cw[DI:], cw[:DI]]).reshape(9, P, TAPS).transpose(1, 0, 2).reshape(P, 9 * TAPS)
        cb = cols(np.concatenate([cb[DI:], cb[:DI]]))
        rep = P // NH
        prm.append(np.concatenate([
            cw, cb, cols(np.repeat(g["L0_attn_D"][n], NS)), cols(g["L0_attn_rms_w"][n]),
            cols(g["L0_attn_ln_w"][n]), cols(g["L0_attn_ln_b"][n]),
            np.tile(g["L0_attn_A_log"][n], rep)[:, None], np.tile(g["L0_attn_dt_bias"][n], rep)[:, None]], axis=1))
    x = g["L0_attn_x"]
    return {
        "x": x.reshape(-1, DM),
        "in_w": np.stack(in_w), "out_w": np.stack(out_w), "prm": np.stack(prm),
        "w3": np.stack([tiles(g[k].T) for k in ("L0_ffn_W_r", "L0_ffn_W_k", "L0_ffn_W_v")]),
        "fprm": np.concatenate([cols(g["L0_ffn_mu_r"]), cols(g["L0_ffn_mu_k"])], axis=1),
        "cT": g["L0_c"].T.reshape(KD, P, -1).transpose(1, 0, 2),
        "wmod": tiles(g["L0_wmod"]),
        "cst": shape_constants(),
    }


def kernel(**inputs):
    import concourse.bacc as _bacc
    from concourse import mybir as _mybir
    from concourse.bass_utils import run_bass_kernel_spmd as _run

    nc = _bacc.Bacc("TRN2", target_bir_lowering=False, num_devices=1)
    arrays, args = {}, []
    for name, a in layout(inputs).items():
        a = np.ascontiguousarray(a)
        arrays[f"in_{name}"] = a
        args.append(nc.dram_tensor(f"in_{name}", a.shape, _mybir.dt.from_np(a.dtype), kind="ExternalInput").ap())
    shape = inputs["L0_attn_x"].shape
    args.append(nc.dram_tensor("out_0", (shape[0] * shape[1], DM), F32, kind="ExternalOutput").ap())
    build(nc, *args, shape[0])
    r = _run(nc, [arrays], core_ids=[0])
    return r.results[0]["out_0"].reshape(shape)
```

```python
from contextlib import ExitStack

import numpy as np

import concourse.bass as bass
from concourse import mybir

ALU = mybir.AluOpType
ACT = mybir.ActivationFunctionType
F32 = mybir.dt.float32
F32R = mybir.dt.float32r

P = 128
DM = 512
DI = 1024
NS = 64
NH = DI // NS
NL = 2
KD = DM // P
KI = DI // P
CH = 64
TB = 256
NB = 4
NPAIR = TB // P
WIN = 2 * P + 2 * DI
TAPS = 4
NG = WIN // (2 * P)
NX = KI // 2
Z_AT = [1, 2, 4, 7]
X_AT = [3, 5, 6, 8]
EPS = 1e-5
MINUS_BIG = -1e30

C_CW = 0
C_CB = C_CW + 9 * TAPS
C_D = C_CB + 9
C_RMS = C_D + KI
C_LNW = C_RMS + KI
C_LNB = C_LNW + KD
C_ALOG = C_LNB + KD
C_DTB = C_ALOG + 1
NPRM = C_DTB + 1

K_RHS = 0
K_LHS = K_RHS + NH * CH
K_ID = K_LHS + TB // CH * P
K_SCAN = K_ID + P
K_DELTA = K_SCAN + P
K_LOW = K_DELTA + NH
K_ONE = K_LOW + 1
K_HALF = K_ONE + 1
K_EPS = K_HALF + 2
K_BLK = K_EPS + 2
NCST = K_BLK + 2


def shape_constants():
    c = np.zeros((P, NCST), np.float32)
    p = np.arange(P)
    h, t = np.arange(NH), np.arange(CH)
    rhs = np.zeros((P, NH, CH), np.float32)
    rhs[32:64] = (p[32:64, None] % NH == h[None, :])[:, :, None]
    rhs[64:] = np.where(t[None, :] < np.arange(CH)[:, None], MINUS_BIG, 0.0)[:, None, :]
    c[:, K_RHS:K_LHS] = rhs.reshape(P, -1)
    lhs = np.zeros((P, TB // CH, P), np.float32)
    lhs[0:32] = 1.0
    for k in range(TB // CH):
        tok = (k % 2) * CH
        lhs[64:, k, tok:tok + CH] = np.eye(CH, dtype=np.float32)
    c[:, K_LHS:K_ID] = lhs.reshape(P, -1)
    c[:, K_ID:K_SCAN] = np.eye(P, dtype=np.float32)
    c[:, K_SCAN:K_DELTA] = (np.arange(P) % CH != 0)[None, :]
    c[:, K_DELTA:K_LOW] = p[:, None] % NH == h[None, :]
    c[:, K_LOW] = (p // NH) % 2
    c[:, K_ONE] = 1.0
    c[:, K_HALF:K_EPS] = -0.5
    c[:, K_EPS:K_BLK] = EPS
    c[:, K_BLK:NCST] = p[:, None] // CH == np.arange(2)[None, :]
    return c


def modulation(nc, sems, cT, wmod, cst, mod_dram, cols_dram, nseq):
    with ExitStack() as ctx:
        def sb(name, shape, dt=F32):
            return ctx.enter_context(nc.sbuf_tensor(name, shape, dt))

        def sem(name):
            return sems(name)

        c_sb = sb("m_c", [P, KD, nseq])
        sc_sb = sb("m_sc", [P, KD, nseq])
        w_sb = sb("m_w", [P, KD, 6 * DM])
        mod_sb = sb("m_mod", [nseq, 6, DM])
        mag_sb = sb("m_mag", [nseq, 6, DM])
        sgn_sb = sb("m_sgn", [nseq, 6, DM])
        id_sb = sb("m_id", [P, P])
        cols_sb = sb("m_cols", [P, nseq, 2 * KD])
        ps = ctx.enter_context(nc.psum_tensor("m_ps", [P, 6, DM], F32))
        ps_c = ctx.enter_context(nc.psum_tensor("m_psc", [P, 2 * KD, nseq], F32))
        turned, cols_done = sem("m_turned"), sem("m_cols_done")
        c_loaded, w_loaded, c_silu, mod_done = sem("m_cl"), sem("m_wl"), sem("m_silu"), sem("m_mm")
        copied, mag_done, sgn_done, post_done, stored = (
            sem("m_cp"), sem("m_mg"), sem("m_sg"), sem("m_post"), sem("m_st"))
        block = ctx.enter_context(nc.Block())

        @block.sync
        def _(sp):
            sp.dma_start(c_sb[:], cT).then_inc(c_loaded, 16)
            sp.dma_start(w_sb[:], wmod).then_inc(w_loaded, 16)
            sp.dma_start(id_sb[:], cst[:, K_ID:K_ID + P]).then_inc(w_loaded, 16)
            sp.wait_ge(post_done, 4)
            sp.dma_start(mod_dram.rearrange("b (s d) -> b s d", s=6), mod_sb[:]).then_inc(stored, 16)
            sp.wait_ge(cols_done, 1)
            sp.dma_start(cols_dram.rearrange("b p k -> p b k"), cols_sb[:]).then_inc(stored, 16)
            sp.wait_ge(stored, 32)

        @block.scalar
        def _(act):
            act.wait_ge(c_loaded, 16)
            nc.scalar.activation(sc_sb[:], c_sb[:], ACT.Silu).then_inc(c_silu, 1)

        @block.tensor
        def _(pe):
            pe.wait_ge(c_silu, 1)
            pe.wait_ge(w_loaded, 32)
            for n in range(6):
                for k in range(KD):
                    last = nc.tensor.matmul(ps[0:nseq, n, :], sc_sb[:, k, :], w_sb[:, k, n * DM:(n + 1) * DM],
                                            start=(k == 0), stop=(k == KD - 1))
            last.then_inc(mod_done, 1)
            pe.wait_ge(post_done, 4)
            for k in range(2 * KD):
                last = nc.tensor.transpose(ps_c[:, k, :], mod_sb[:, 3 + k // KD, (k % KD) * P:(k % KD + 1) * P],
                                           id_sb[0:nseq, 0:nseq])
            last.then_inc(turned, 1)

        @block.vector
        def _(dve):
            dve.wait_ge(mod_done, 1)
            nc.vector.tensor_copy(mod_sb[:], ps[0:nseq]).then_inc(copied, 1)
            dve.wait_ge(copied, 1)
            for n in (1, 4):
                nc.vector.tensor_scalar_add(mod_sb[:, n, :], mod_sb[:, n, :], 1.0).then_inc(post_done, 1)
            for k, n in enumerate((2, 5)):
                g = mod_sb[:, n, :]
                nc.vector.tensor_scalar_mul(mag_sb[:, n, :], g, -1.0).then_inc(mag_done, 1)
                nc.vector.tensor_scalar(sgn_sb[:, n, :], g, 0.0, 2.0, ALU.is_ge, ALU.mult).then_inc(sgn_done, 1)
                dve.wait_ge(mag_done, 3 * k + 1)
                nc.vector.tensor_tensor(mag_sb[:, n, :], mag_sb[:, n, :], g, ALU.max).then_inc(mag_done, 1)
                dve.wait_ge(mag_done, 3 * k + 2)
                nc.vector.tensor_scalar_max(mag_sb[:, n, :], mag_sb[:, n, :], 0.25).then_inc(mag_done, 1)
                dve.wait_ge(mag_done, 3 * k + 3)
                dve.wait_ge(sgn_done, k + 1)
                nc.vector.scalar_tensor_tensor(out=g, in0=sgn_sb[:, n, :], scalar=-1.0, in1=mag_sb[:, n, :],
                                               op0=ALU.add, op1=ALU.mult).then_inc(post_done, 1)
            dve.wait_ge(turned, 1)
            nc.vector.tensor_copy(cols_sb[:].rearrange("p b k -> p k b"), ps_c[:]).then_inc(cols_done, 1)


def mamba_layer(nc, sems, layer, src, dst, in_w, out_w, prm, cst, mod_dram, nseq):
    first = layer == 0
    b0 = layer * nseq
    with ExitStack() as ctx:
        def sb(name, shape, dt=F32):
            return ctx.enter_context(nc.sbuf_tensor(f"l{layer}_{name}", shape, dt))

        def psum(name, shape):
            return ctx.enter_context(nc.psum_tensor(f"l{layer}_{name}", shape, F32))

        def sem(name):
            return sems("l_" + name)

        wi_hi, wi_lo = sb("wi_hi", [P, KD, WIN], F32R), sb("wi_lo", [P, KD, WIN], F32R)
        wo_hi, wo_lo = sb("wo_hi", [P, KI, DM], F32R), sb("wo_lo", [P, KI, DM], F32R)
        prm_sb = sb("prm", [P, NPRM])
        small = sb("small", [P, NCST - K_ID])
        a_neg = sb("a_neg", [P, 1])
        hn = sb("hn", [P, NPAIR, DM])
        res = sb("res", [P, NPAIR, DM])
        v = sb("v", [P, 2, TB])
        u_hi, u_lo = sb("u_hi", [P, KD, TB], F32R), sb("u_lo", [P, KD, TB], F32R)
        raw = sb("raw", [P, 2, TB + TAPS - 1])
        acc_bc = v[:, 0, :]
        halo = sb("halo", [P, 9, TAPS - 1])
        xc = sb("xc", [P, KI, TB])
        zs = sb("zs", [P, 2, KI, TB])
        bti = sb("bti", [NS, TB // CH, P])
        bt, ct = sb("bt", [NS, TB]), sb("ct", [NS, TB])
        dt = sb("dt", [P, 2, TB])
        dtx = sb("dtx", [P, TB])
        dty = sb("dty", [P, TB])
        cum = sb("cum", [P, 2, TB])
        lhs = sb("lhs", [P, TB // CH, P], F32R)
        rhs = sb("rhs", [P, NH, CH], F32R)
        misc = sb("misc", [P, 4, 64])
        bd = sb("bd", [P, P])
        xs = sb("xs", [P, 2, DI])
        xw = sb("xw", [P, DI])
        e = sb("e", [P, 2, NH, CH])
        dec = sb("dec", [P, 2, NH])
        g = sb("g", [P, NPAIR, KI, P])
        g_hi, g_lo = sb("g_hi", [P, KI, P], F32R), sb("g_lo", [P, KI, P], F32R)
        ms = sb("ms", [P, 1])
        rr = sb("rr", [P, 1])
        spare = sb("spare", [P, 1])
        stats = sb("stats", [P, NPAIR, 6])
        mv = sb("mv", [P, NPAIR, 2])
        rstd = sb("rstd", [P, NPAIR])
        if first:
            mod = sb("mod", [P, 2, DM])

        ring = psum("ring", [P, 2, 512])
        wide = psum("wide", [P, 2, DI])
        ps_y = psum("ps_y", [P, KI, CH])
        ps_m = psum("ps_m", [P, 512])

        rounds = 2 if first else 1

        def norm_round(i, rnd):
            return 2 * i + rnd if first else i + NB * nseq

        def const(a, n):
            return small[:, a - K_ID:a - K_ID + n]

        ident, one = const(K_ID, P), const(K_ONE, 1)
        s_cst, s_prm = sem("cst"), sem("prm")
        s_stage = [sem("stage0"), sem("stage1")]
        s_whi, s_wlo, s_wsc = sem("w_hi"), sem("w_lo"), sem("w_scaled")
        s_init, s_aexp, s_aneg, s_cst_copy = sem("init"), sem("a_exp"), sem("a_neg"), sem("cst_copy")
        s_load = sem("load")
        s_res = [sem("res0"), sem("res1")]
        s_store = [sem("store0"), sem("store1")]
        s_h0 = sem("h0_stored")
        s_mod = sem("mod")
        s_bn, s_mv, s_var, s_rstd, s_norm, s_modm, s_moda = (
            sem("bn"), sem("mv"), sem("var"), sem("rstd"), sem("norm"), sem("mod_mul"), sem("mod_add"))
        s_ut, s_utev, s_v, s_uhi, s_ulo = sem("u_T"), sem("u_T_read"), sem("v"), sem("u_hi"), sem("u_lo")
        s_in, s_inev = sem("proj"), sem("proj_read")
        s_xb, s_abs, s_exp, s_ln, s_dt = sem("dt_x"), sem("dt_abs"), sem("dt_exp"), sem("dt_ln"), sem("dt")
        s_a, s_cum, s_vr, s_lhs, s_dend, s_wexp, s_td = (
            sem("dta"), sem("cum"), sem("cum_parts"), sem("lhs"), sem("d_end"), sem("w_exp"),
            sem("dt_w"))
        s_halo, s_raw, s_halo2, s_acc0, s_acc, s_bc, s_xc = (
            sem("halo"), sem("raw"), sem("halo2"), sem("acc0"), sem("acc"), sem("bc"), sem("xc"))
        s_tap, s_zs = sem("tap"), sem("zs")
        s_rhs, s_arg, s_e, s_dec, s_m = sem("rhs"), sem("arg"), sem("e"), sem("dec"), sem("m")
        s_mp, s_mev, s_bd = sem("misc_ps"), sem("misc"), sem("bd")
        s_xp, s_xev, s_sps = sem("x_T"), sem("x_T_read"), sem("state_ps")
        s_sd, s_st = sem("sd"), sem("state")
        s_y, s_yev, s_dx, s_gate = sem("y"), sem("y_read"), sem("dx"), sem("gate")
        s_ghi, s_glo, s_sq, s_sum = sem("g_hi"), sem("g_lo"), sem("g_sq"), sem("g_sum")
        s_ss, s_ms, s_ms2, s_rr, s_o, s_out = sem("ss"), sem("ms"), sem("ms2"), sem("rr"), sem("o"), sem("out")

        block = ctx.enter_context(nc.Block())

        pieces = [("in", k, n * (WIN // 2), WIN // 2) for k in range(KD) for n in range(2)]
        pieces += [("out", k, 0, 2 * DM) for k in range(0, KI, 2)]
        stage = [zs[:, k].rearrange("p k t -> p (k t)") for k in range(2)]

        def piece_at(n, whole_in, whole_out):
            kind, k, c0, w = pieces[n]
            if kind == "in":
                return whole_in[:, k, c0:c0 + w]
            return whole_out[:, k:k + 2, :].rearrange("p k n -> p (k n)")

        def loop(eng, body):
            if first:
                for s in range(NB):
                    body(0, s, True, True)
            with eng.Fori(b0 + first, b0 + nseq - 1) as b:
                for s in range(NB):
                    body(b, s, True, True)
            for s in range(NB):
                body(b0 + nseq - 1, s, s < NB - 1, s < NB - 2)

        def ahead(b, s, n):
            return (b + 1, s + n - NB) if s + n >= NB else (b, s + n)

        def at_least_0(count):
            return max(count, 0) if isinstance(count, int) else count

        USE_P = [0, 1, 2, 3, 4, 5, 7, 8, 9]
        USE_O = [6, 12]
        USE_T = [10, 11]
        ring_uses = 13

        def bank(s, use):
            return (ring_uses * s + use) % 2

        @block.sync
        def _(sp):
            sp.dma_start(e[:].rearrange("p a h t -> p (a h t)")[:, 0:K_ID], cst[:, 0:K_ID]).then_inc(s_cst, 16)
            sp.dma_start(small[:], cst[:, K_ID:NCST]).then_inc(s_cst, 16)
            sp.dma_start(prm_sb[:], prm).then_inc(s_prm, 16)

            def load(b, s):
                i = NB * b + s
                sp.wait_ge(s_ut, 2 * i)
                sp.dma_start(hn[:], src[bass.ds((i - NB * b0) * TB, TB), :].rearrange("(t p) d -> p t d", p=P)
                             ).then_inc(s_load, 16)

            def load_mod(b):
                sp.wait_ge(s_moda, NB * NPAIR * b)
                sp.dma_start(mod[:], mod_dram[bass.ds(b, 1), 0:2 * DM].rearrange("o (s d) -> o s d", s=2)
                             .broadcast_to([P, 2, DM])).then_inc(s_mod, 16)

            def store_modulated(b, s):
                i = NB * b + s
                sp.wait_ge(s_moda, NPAIR * (i + 1))
                sp.dma_start(dst[bass.ds(i * TB, TB), :].rearrange("(t p) d -> p t d", p=P), hn[:]
                             ).then_inc(s_h0, 16)

            if first:
                load_mod(b0)
            load(b0, 0)
            for n, (kind, k, c0, w) in enumerate(pieces):
                if n >= 2:
                    sp.wait_ge(s_wlo, len(pieces) * layer + n - 1)
                source = in_w[:, k, c0:c0 + w] if kind == "in" else out_w[:, k:k + 2, :].rearrange("p k n -> p (k n)")
                sp.dma_start(stage[n % 2][:, 0:w], source).then_inc(s_stage[n % 2], 16)
            if first:
                store_modulated(b0, 0)
            load(b0, 1)
            if first:
                store_modulated(b0, 1)

            def body(b, s, n1, n2):
                i = NB * b + s
                if n2:
                    if first and s + 2 == NB:
                        load_mod(b + 1)
                    load(*ahead(b, s, 2))
                row = (i - NB * b0) * TB
                for j in range(NPAIR):
                    if first and not n2:
                        sp.wait_ge(s_h0, 16 * (i + 1))
                    sp.wait_ge(s_store[j], 16 * i)
                    sp.dma_start(res[:, j], (dst if first else src)[bass.ds(row + j * P, P), :]
                                 ).then_inc(s_res[j], 16)
                if n2 and first:
                    store_modulated(*ahead(b, s, 2))
                for j in range(NPAIR):
                    sp.wait_ge(s_out, NPAIR * i + j + 1)
                    sp.dma_start(dst[bass.ds(row + j * P, P), :], res[:, j]).then_inc(s_store[j], 16)

            loop(sp, body)
            for k in range(NPAIR):
                sp.wait_ge(s_store[k], 16 * NB * (b0 + nseq))

        @block.tensor
        def _(pe):
            def products(out, pairs):
                n = 3 * len(pairs)
                k = 0
                for (a_hi, a_lo), (b_hi, b_lo) in pairs:
                    for a, c in ((a_lo, b_hi), (a_hi, b_lo), (a_hi, b_hi)):
                        last = nc.tensor.matmul(out, a, c, start=(k == 0), stop=(k == n - 1))
                        k += 1
                return last

            def input_T(b, s, banks, read):
                i = NB * b + s
                pe.wait_ge(s_norm, NPAIR * norm_round(i + 1, 0))
                for half in range(2):
                    if read is not None:
                        pe.wait_ge(s_inev, read - 1 + half)
                    out = ring[:, banks[half], :].rearrange("p (k t) -> p k t", k=2)
                    for k in range(2):
                        for t in range(NPAIR):
                            d = (2 * half + k) * P
                            last = nc.tensor.transpose(out[:, k, t * P:(t + 1) * P], hn[:, t, d:d + P], ident)
                    last.then_inc(s_ut, 1)

            def project(b, s, n, bk):
                if n == 0:
                    pe.wait_ge(s_ulo, 2 * (NB * b + s + 1))
                for t in range(2):
                    c = (2 * n + t) * P
                    last = products(ring[:, bk, t * TB:(t + 1) * TB],
                                    [((wi_hi[:, k, c:c + P], wi_lo[:, k, c:c + P]), (u_hi[:, k, :], u_lo[:, k, :]))
                                     for k in range(KD)])
                last.then_inc(s_in, 1)

            def front(b, s, j):
                i = NB * b + s
                q = NPAIR * i + j
                if j == 0:
                    pe.wait_ge(s_bc, 2 * (i + 1))
                    pe.wait_ge(s_td, i + 1)
                    pe.wait_ge(s_ms, q)
                else:
                    pe.wait_ge(s_mev, q)
                for k in range(2):
                    c = 2 * j + k
                    nc.tensor.matmul(ps_m[:, 128 + 64 * k:192 + 64 * k], bti[:, c, :],
                                     ct[:, c * CH:(c + 1) * CH], start=True, stop=True)
                nc.tensor.transpose(ps_m[:, 0:64], bt[:, j * P:(j + 1) * P], ident[0:NS, 0:NS])
                nc.tensor.transpose(ps_m[:, 64:128], dt[0:64, s % 2, j * P:(j + 1) * P], ident[0:NS, 0:NS]
                                    ).then_inc(s_mp, 1)
                if j == 0:
                    pe.wait_ge(s_xc, NX * (i + 1))
                pe.wait_ge(s_e, 2 * q)
                for k in range(KI):
                    last = nc.tensor.transpose(wide[:, 0, k * P:(k + 1) * P], xc[:, k, j * P:(j + 1) * P], ident)
                last.then_inc(s_xp, 1)

            def exponents(b, s, j, odd):
                i = NB * b + s
                q = NPAIR * i + j
                c = 2 * j + odd
                if odd:
                    pe.wait_ge(s_xev, 3 * (q + 1))
                else:
                    pe.wait_ge(s_st, 2 * q)
                pe.wait_ge(s_rhs, 2 * q + odd + 1)
                for n in range(2):
                    last = nc.tensor.matmul(wide[:, 0 if odd else 1, n * 512:(n + 1) * 512], lhs[:, c, :],
                                            rhs[:].rearrange("p h t -> p (h t)")[:, n * 512:(n + 1) * 512],
                                            start=True, stop=True)
                last.then_inc(s_arg, 1)

            def outputs(b, s, j, odd):
                q = NPAIR * (NB * b + s) + j
                pe.wait_ge(s_m, 2 * q + odd + 1)
                if odd:
                    pe.wait_ge(s_st, 2 * q + 1)
                else:
                    pe.wait_ge(s_xev, 3 * (q + 1))
                pe.wait_ge(s_yev, 2 * q + odd)
                for h in range(NH):
                    r = (h % 2) * NS
                    last = nc.tensor.matmul(ps_y[r:r + NS, h // 2, :], xs[:, odd, h * NS:(h + 1) * NS],
                                            e[:, odd, h, :], start=True, stop=True)
                last.then_inc(s_y, 1)

            def states(b, s, j):
                q = NPAIR * (NB * b + s) + j
                pe.wait_ge(s_bd, q + 1)
                pe.wait_ge(s_e, 2 * q + 1)
                for n in range(2):
                    last = nc.tensor.matmul(wide[:, 1, n * 512:(n + 1) * 512], bd[:], xw[:, n * 512:(n + 1) * 512],
                                            start=True, stop=True)
                last.then_inc(s_sps, 1)

            def out_product(b, s, j, bk):
                q = NPAIR * (NB * b + s) + j
                if j == 0:
                    pe.wait_ge(s_mev, q + 2)
                else:
                    pe.wait_ge(s_ms, q)

                pe.wait_ge(s_glo, q + 1)
                products(ring[:, bk, :], [((g_hi[:, k, :], g_lo[:, k, :]), (wo_hi[:, k, :], wo_lo[:, k, :]))
                                          for k in range(KI)]).then_inc(s_o, 1)
                pe.wait_ge(s_sum, 3 * (q + 1))
                nc.tensor.matmul(ps_m[:, 0:1], g[:, j, 0, :], one, start=True, stop=True).then_inc(s_ss, 1)

            pe.wait_ge(s_cst, 32 * (layer + 1))
            pe.wait_ge(s_wlo, len(pieces) * (layer + 1))
            pe.wait_ge(s_init, 2 * (layer + 1))
            pe.wait_ge(s_cst_copy, 3 * (layer + 1))
            input_T(b0, 0, (bank(-2, USE_T[0]), bank(-2, USE_T[1])), None)
            for n in range(NG):
                k = NG * NB * b0 + n
                if n >= 2:
                    pe.wait_ge(s_inev, k if n == 6 else k - 1)
                project(b0, 0, n, bank(-1, USE_P[n]))
            input_T(b0, 1, (bank(-1, USE_T[0]), bank(-1, USE_T[1])), NG * (NB * b0 + 1))

            def body(b, s, n1, n2):
                i = NB * b + s
                nxt = ahead(b, s, 1)

                def proj(n):
                    if not n1:
                        return
                    if n == 1:
                        pe.wait_ge(s_out, NPAIR * i)
                    elif n == 7:
                        pe.wait_ge(s_out, NPAIR * i + 1)
                    elif n >= 2:
                        pe.wait_ge(s_inev, NG * (i + 1) + {6: 6, 8: 7}.get(n, n - 1))
                    project(*nxt, n, bank(s, USE_P[n]))

                front(b, s, 0)
                exponents(b, s, 0, 0)
                proj(0)
                proj(1)
                outputs(b, s, 0, 0)
                exponents(b, s, 0, 1)
                states(b, s, 0)
                proj(2)
                outputs(b, s, 0, 1)
                front(b, s, 1)
                exponents(b, s, 1, 0)
                proj(3)
                proj(4)
                proj(5)
                outputs(b, s, 1, 0)
                exponents(b, s, 1, 1)
                states(b, s, 1)
                if n1:
                    pe.wait_ge(s_inev, NG * (i + 1) + 5)
                out_product(b, s, 0, bank(s, USE_O[0]))
                outputs(b, s, 1, 1)
                for n in (6, 7, 8):
                    proj(n)
                if n2:
                    input_T(*ahead(b, s, 2), (bank(s, USE_T[0]), bank(s, USE_T[1])), NG * (i + 2))
                    pe.wait_ge(s_utev, 2 * (i + 2) + 1)
                elif n1:
                    pe.wait_ge(s_inev, NG * (i + 2) - 1)
                else:
                    pe.wait_ge(s_out, NPAIR * i + 1)
                out_product(b, s, 1, bank(s, USE_O[1]))

            loop(pe, body)

        @block.scalar
        def _(act):
            act.wait_ge(s_prm, 16 * (layer + 1))
            act.wait_ge(s_cst, 32 * (layer + 1))
            nc.scalar.activation(a_neg[:], prm_sb[:, C_ALOG:C_ALOG + 1], ACT.Exp).then_inc(s_aexp, 1)
            for n, (kind, k, c0, w) in enumerate(pieces):
                act.wait_ge(s_stage[n % 2], 16 * (len(pieces) // 2 * layer + n // 2 + 1))
                st = stage[n % 2][:, 0:w]
                if kind == "out":
                    for m in range(2):
                        r = C_RMS + k + m
                        nc.scalar.activation(st[:, m * DM:(m + 1) * DM], st[:, m * DM:(m + 1) * DM], ACT.Identity,
                                             scale=prm_sb[:, r:r + 1]).then_inc(s_wsc, 1)
                    act.wait_ge(s_wsc, KI * layer + k + 2)
                nc.scalar.activation(piece_at(n, wi_hi, wo_hi), st, ACT.Identity).then_inc(s_whi, 1)

            def u_read(b, s, halves):
                i = NB * b + s
                if 0 in halves:
                    act.wait_ge(s_in, NG * i)
                    act.wait_ge(s_bc, 2 * i)
                for half in halves:
                    act.wait_ge(s_ut, 2 * i + half + 1)
                    act.wait_ge(s_ulo, 2 * i + half)
                    for k in range(2):
                        d = 2 * half + k
                        nc.scalar.activation(
                            v[:, k, :], ring[:, bank(s - 2, USE_T[half]), k * TB:(k + 1) * TB], ACT.Identity,
                            bias=prm_sb[:, C_LNB + d:C_LNB + d + 1], scale=prm_sb[:, C_LNW + d:C_LNW + d + 1]
                        ).then_inc(s_utev if k == 1 else s_v, 1)
                    act.wait_ge(s_utev, 2 * i + half + 1)
                    nc.scalar.activation(u_hi[:, 2 * half:2 * half + 2, :], v[:], ACT.Identity).then_inc(s_uhi, 1)

            def step_exp(b, s):
                i = NB * b + s
                act.wait_ge(s_in, NG * i + 1)
                act.wait_ge(s_td, i)
                nc.scalar.activation(dtx[:], ring[:, bank(s - 1, USE_P[0]), 0:TB], ACT.Identity,
                                     bias=prm_sb[:, C_DTB:C_DTB + 1]).then_inc(s_xb, 1)
                act.wait_ge(s_xb, i + 1)
                nc.scalar.activation(dty[:], dtx[:], ACT.Abs).then_inc(s_abs, 1)
                act.wait_ge(s_abs, i + 1)
                nc.scalar.activation(dty[:], dty[:], ACT.Exp, scale=-1.0).then_inc(s_exp, 1)
                act.wait_ge(s_exp, i + 1)
                nc.scalar.activation(dty[:], dty[:], ACT.Ln, bias=1.0).then_inc(s_ln, 1)

            def step_decay(b, s):
                act.wait_ge(s_dend, NB * b + s + 1)
                nc.scalar.activation(dty[:], dty[:], ACT.Exp).then_inc(s_wexp, 1)

            def conv_in(b, s, c):
                i = NB * b + s
                m = (NX + 1) * i + c
                n = 0 if c == 0 else X_AT[c - 1]
                t0, nt = (0, 1) if c == 0 else (2 * c - 1, 2)
                act.wait_ge(s_in, NG * i + n + 1)
                src_ps = ring[:, bank(s - 1, USE_P[n]), (2 - nt) * TB:].rearrange("p (k t) -> p k t", k=nt)
                act.wait_ge(s_acc, m)
                if s == 0:
                    nc.scalar.mul(raw[:, 0:nt, 0:TAPS - 1], small[:, 0:nt * 3].rearrange("p (k t) -> p k t", k=nt),
                                  0.0).then_inc(s_halo, 1)
                else:
                    act.wait_ge(s_halo2, m - (NX + 1) + 1)
                    nc.scalar.copy(raw[:, 0:nt, 0:TAPS - 1], halo[:, t0:t0 + nt, :]).then_inc(s_halo, 1)
                act.wait_ge(s_halo, m + 1)
                nc.scalar.copy(halo[:, t0:t0 + nt, :], src_ps[:, :, TB - TAPS + 1:]).then_inc(s_halo2, 1)
                nc.scalar.copy(raw[:, 0:nt, TAPS - 1:], src_ps).then_inc(s_inev, 1)
                act.wait_ge(s_inev, NG * i + n + 1)
                if c == 0:
                    act.wait_ge(s_ulo, 2 * (i + 1))
                elif c == 1:
                    act.wait_ge(s_dx, NPAIR * i)
                    act.wait_ge(s_xp, NPAIR * i)
                for k in range(nt):
                    w, bb = C_CW + (t0 + k) * TAPS, C_CB + t0 + k
                    ins = nc.scalar.activation(acc_bc if c == 0 else xc[:, t0 - 1 + k, :], raw[:, k, 0:TB],
                                               ACT.Identity, bias=prm_sb[:, bb:bb + 1],
                                               scale=prm_sb[:, w:w + 1])
                ins.then_inc(s_acc0, 1)

            def silu_bc(b, s):
                i = NB * b + s
                act.wait_ge(s_acc, (NX + 1) * i + 1)
                act.wait_ge(s_mp, NPAIR * i)
                view = bti[:].rearrange("n (q c) (a t) -> n q (c a) t", c=2, a=2)[:, :, 0::3, :]
                nc.scalar.activation(view, acc_bc[0:NS, :].rearrange("n (q c t) -> n q c t", c=2, t=CH),
                                     ACT.Silu)
                nc.scalar.activation(bt[:], acc_bc[0:NS, :], ACT.Silu).then_inc(s_bc, 1)
                nc.scalar.activation(ct[:], acc_bc[NS:P, :], ACT.Silu).then_inc(s_bc, 1)

            def silu_x(b, s, c):
                act.wait_ge(s_acc, (NX + 1) * (NB * b + s) + c + 1)
                x = xc[:, 2 * c - 2:2 * c, :]
                nc.scalar.activation(x, x, ACT.Silu).then_inc(s_xc, 1)

            def z_read(b, s, k):
                i = NB * b + s
                n = Z_AT[k]
                act.wait_ge(s_in, NG * i + n + 1)
                if k == 0:
                    act.wait_ge(s_gate, at_least_0(NPAIR * (i - 1)))
                nc.scalar.copy(zs[:, s % 2, 2 * k:2 * k + 2, :], ring[:, bank(s - 1, USE_P[n]), :]
                               .rearrange("p (k t) -> p k t", k=2)).then_inc(s_inev, 1)

            def silu_z(b, s):
                act.wait_ge(s_inev, NG * (NB * b + s) + Z_AT[-1] + 1)
                nc.scalar.activation(zs[:, s % 2], zs[:, s % 2], ACT.Silu).then_inc(s_zs, 1)

            def pair_small(b, s, j):
                q = NPAIR * (NB * b + s) + j
                act.wait_ge(s_mp, q + 1)
                act.wait_ge(s_m, 2 * q)
                act.wait_ge(s_bd, q)
                nc.scalar.copy(misc[:].rearrange("p a t -> p (a t)"), ps_m[:, 0:256]).then_inc(s_mev, 1)

            def decays(b, s, j, odd):
                q = NPAIR * (NB * b + s) + j
                act.wait_ge(s_arg, 2 * q + odd + 1)
                nc.scalar.activation(e[:, odd].rearrange("p h t -> p (h t)"), wide[:, 0 if odd else 1, :],
                                     ACT.Exp).then_inc(s_e, 1)

            def high_g(b, s, j):
                q = NPAIR * (NB * b + s) + j
                act.wait_ge(s_gate, q + 1)
                act.wait_ge(s_o, q)
                nc.scalar.activation(g_hi[:], g[:, j], ACT.Identity).then_inc(s_ghi, 1)

            def square_g(b, s, j):
                q = NPAIR * (NB * b + s) + j
                act.wait_ge(s_glo, q + 1)
                nc.scalar.activation(g[:, j], g[:, j], ACT.Square).then_inc(s_sq, 1)

            def body(b, s, n1, n2):
                nxt = ahead(b, s, 1)
                pair_small(b, s, 0)
                decays(b, s, 0, 0)
                if n1:
                    step_exp(*nxt)
                    conv_in(*nxt, 0)
                    z_read(*nxt, 0)
                decays(b, s, 0, 1)
                if n1:
                    z_read(*nxt, 1)
                pair_small(b, s, 1)
                decays(b, s, 1, 0)
                if n1:
                    step_decay(*nxt)
                    conv_in(*nxt, 1)
                high_g(b, s, 0)
                if n1:
                    z_read(*nxt, 2)
                square_g(b, s, 0)
                if n1:
                    conv_in(*nxt, 2)
                decays(b, s, 1, 1)
                if n1:
                    silu_bc(*nxt)
                    silu_x(*nxt, 1)
                if n1:
                    conv_in(*nxt, 3)
                    silu_x(*nxt, 2)
                    z_read(*nxt, 3)
                high_g(b, s, 1)
                if n1:
                    conv_in(*nxt, 4)
                if n2:
                    u_read(*ahead(b, s, 2), (0,))
                square_g(b, s, 1)
                if n1:
                    silu_x(*nxt, 3)
                if n2:
                    u_read(*ahead(b, s, 2), (1,))
                if n1:
                    silu_x(*nxt, 4)
                    silu_z(*nxt)

            u_read(b0, 0, (0, 1))
            step_exp(b0, 0)
            conv_in(b0, 0, 0)
            step_decay(b0, 0)
            for n in range(1, NG):
                if n in Z_AT:
                    z_read(b0, 0, Z_AT.index(n))
                else:
                    conv_in(b0, 0, X_AT.index(n) + 1)
                if n == 1:
                    silu_bc(b0, 0)
                if n in X_AT:
                    silu_x(b0, 0, X_AT.index(n) + 1)
            silu_z(b0, 0)
            u_read(b0, 1, (0, 1))
            loop(act, body)

        @block.vector
        def _(dve):
            dve.wait_ge(s_cst, 32 * (layer + 1))
            stage_c = e[:].rearrange("p a h t -> p (a h t)")
            nc.vector.tensor_copy(rhs[:].rearrange("p h t -> p (h t)"), stage_c[:, K_RHS:K_LHS]).then_inc(s_cst_copy, 1)
            nc.vector.tensor_copy(lhs[:].rearrange("p c t -> p (c t)"), stage_c[:, K_LHS:K_ID]).then_inc(s_cst_copy, 1)
            eye = bti[:].rearrange("n c (a t) -> n (c a) t", a=2)
            for pr in range(2):
                ins = nc.vector.tensor_copy(eye[:, 4 * pr + 1:4 * pr + 3, :],
                                            ident[0:NS, 0:NS].unsqueeze(1).broadcast_to([NS, 2, NS]))
            ins.then_inc(s_cst_copy, 1)
            nc.vector.memset(xs[:], 0.0).then_inc(s_init, 1)
            nc.vector.memset(dec[:], 0.0).then_inc(s_init, 1)
            dve.wait_ge(s_aexp, layer + 1)
            nc.vector.tensor_scalar_mul(a_neg[:], a_neg[:], -1.0).then_inc(s_aneg, 1)
            for n, (kind, k, c0, w) in enumerate(pieces):
                dve.wait_ge(s_whi, len(pieces) * layer + n + 1)
                nc.vector.tensor_tensor(piece_at(n, wi_lo, wo_lo), stage[n % 2][:, 0:w],
                                        piece_at(n, wi_hi, wo_hi).bitcast(F32), ALU.subtract).then_inc(s_wlo, 1)

            def row_stats(b, s, rnd):
                i = NB * b + s
                m = NPAIR * norm_round(i, rnd)
                if rnd == 0:
                    dve.wait_ge(s_load, 16 * (i + 1))
                else:
                    dve.wait_ge(s_moda, NPAIR * (i + 1))
                dve.wait_ge(s_mv, m)
                for t in range(NPAIR):
                    nc.vector.bn_stats(stats[:, t, :], hn[:, t, :]).then_inc(s_bn, 1)
                dve.wait_ge(s_norm, m)
                dve.wait_ge(s_bn, m + NPAIR)
                nc.vector.memset(spare[:], 0.0)
                for t in range(NPAIR):
                    nc.vector.bn_aggr(mv[:, t, :], stats[:, t, :]).then_inc(s_mv, 1)

            def normalise(b, s, rnd):
                i = NB * b + s
                m = norm_round(i, rnd)
                dve.wait_ge(s_rstd, m + 1)
                if rnd == 1:
                    dve.wait_ge(s_h0, 16 * (i + 1))
                for t in range(NPAIR):
                    nc.vector.tensor_scalar(hn[:, t, :], hn[:, t, :], mv[:, t, 0:1], rstd[:, t:t + 1],
                                            ALU.subtract, ALU.mult).then_inc(s_norm, 1)

            def split_u(b, s):
                i = NB * b + s
                for half in range(2):
                    dve.wait_ge(s_uhi, 2 * i + half + 1)
                    k = slice(2 * half, 2 * half + 2)
                    nc.vector.tensor_tensor(u_lo[:, k, :], v[:], u_hi[:, k, :].bitcast(F32),
                                            ALU.subtract).then_inc(s_ulo, 1)

            def steps(b, s):
                i = NB * b + s
                p = s % 2
                dve.wait_ge(s_ln, i + 1)
                nc.vector.scalar_tensor_tensor(out=dt[:, p], in0=dtx[:], scalar=0.0, in1=dty[:], op0=ALU.max,
                                               op1=ALU.add).then_inc(s_dt, 1)
                dve.wait_ge(s_dt, i + 1)
                nc.vector.tensor_scalar(dtx[:], dt[:, p], a_neg[:], None, ALU.mult).then_inc(s_a, 1)
                dve.wait_ge(s_rhs, at_least_0(2 * NPAIR * (i - 1)))
                dve.wait_ge(s_a, i + 1)
                for j in range(NPAIR):
                    t = slice(j * P, (j + 1) * P)
                    ins = nc.vector.tensor_tensor_scan(cum[:, p, t], const(K_SCAN, P), dtx[:, t], 0.0,
                                                       ALU.mult, ALU.add)
                ins.then_inc(s_cum, 1)
                dve.wait_ge(s_cum, i + 1)
                c4 = cum[:, p].rearrange("p (c t) -> p c t", t=CH)
                nc.vector.tensor_tensor(dty[:].rearrange("p (c t) -> p c t", t=CH),
                                        c4[:, :, CH - 1:CH].broadcast_to([P, TB // CH, CH]), c4,
                                        ALU.subtract).then_inc(s_dend, 1)

            def sum_parts(b, s):
                i = NB * b + s
                p = s % 2
                nc.vector.tensor_copy(dtx[:].bitcast(F32R), cum[:, p]).then_inc(s_vr, 1)
                dve.wait_ge(s_vr, 3 * i + 1)
                nc.vector.tensor_scalar(dtx[:], dtx[:], const(K_LOW, 1), None, ALU.mult).then_inc(s_vr, 1)
                dve.wait_ge(s_dend, i + 1)
                dve.wait_ge(s_vr, 3 * i + 2)
                nc.vector.tensor_tensor(cum[:, p], cum[:, p], dtx[:], ALU.subtract).then_inc(s_vr, 1)

            def step_weights(b, s):
                i = NB * b + s
                dve.wait_ge(s_wexp, i + 1)
                nc.vector.tensor_tensor(dt[32:64, s % 2, :], dt[32:64, s % 2, :], dty[32:64, :], ALU.mult
                                        ).then_inc(s_td, 1)

            def stationary_sums(b, s):
                i = NB * b + s
                dve.wait_ge(s_arg, 2 * NPAIR * i)
                dve.wait_ge(s_vr, 3 * (i + 1))
                lv = lhs[32:64].rearrange("p c (a t) -> p (c a) t", a=2)
                cv = cum[32:64, s % 2].rearrange("p (c t) -> p c t", t=CH)
                for pr in range(2):
                    nc.vector.tensor_scalar(lv[:, 4 * pr:4 * pr + 4:3, :], cv[:, 2 * pr:2 * pr + 2, :], -1.0, None,
                                            ALU.mult).then_inc(s_lhs, 1)

            def taps(b, s, c):
                i = NB * b + s
                t0, nt = (0, 1) if c == 0 else (2 * c - 1, 2)
                dve.wait_ge(s_acc0, (NX + 1) * i + c + 1)
                base = 18 * i + (0 if c == 0 else 2 + 4 * (c - 1))
                for tap in range(1, TAPS):
                    if tap > 1:
                        dve.wait_ge(s_tap, base + (tap - 1) * nt)
                    for k in range(nt):
                        w = C_CW + (t0 + k) * TAPS + tap
                        acc = acc_bc if c == 0 else xc[:, t0 - 1 + k, :]
                        ins = nc.vector.scalar_tensor_tensor(
                            out=acc, in0=raw[:, k, tap:tap + TB], scalar=prm_sb[:, w:w + 1], in1=acc,
                            op0=ALU.mult, op1=ALU.add)
                        if tap < TAPS - 1:
                            ins.then_inc(s_tap, 1)
                ins.then_inc(s_acc, 1)

            def x_read(b, s, j):
                q = NPAIR * (NB * b + s) + j
                dve.wait_ge(s_xp, q + 1)
                dve.wait_ge(s_mev, q + 1)

                def scaled(out, rows, col):
                    pt = wide[rows, 0, :].rearrange("p (h n) -> p h n", n=NS)
                    nc.vector.tensor_tensor(out.rearrange("p (h n) -> p h n", n=NS), pt,
                                            misc[rows, 1, col:col + NH].unsqueeze(2)
                                            .broadcast_to([out.shape[0], NH, NS]), ALU.mult).then_inc(s_xev, 1)

                scaled(xs[0:CH, 0, :], slice(0, CH), 0)
                dve.wait_ge(s_sd, 2 * q)
                dve.wait_ge(s_st, 2 * q)
                scaled(xw[:], slice(0, P), 32)
                dve.wait_ge(s_y, 2 * q)
                scaled(xs[CH:P, 1, :], slice(CH, P), 0)

            def matrices(b, s, j, odd):
                q = NPAIR * (NB * b + s) + j
                n = 2 * q + odd
                dve.wait_ge(s_e, n + 1)
                dve.wait_ge(s_sd, 2 * q)
                rows = slice(0, CH) if odd else slice(CH, P)
                nc.vector.tensor_copy(dec[rows, odd, :], e[rows, odd, :, CH - 1]).then_inc(s_dec, 1)
                dve.wait_ge(s_dec, n + 1)
                dve.wait_ge(s_mev, q + 1)
                nc.vector.tensor_tensor(e[:, odd], e[:, odd],
                                        misc[:, 2 + odd, :].unsqueeze(1).broadcast_to([P, NH, CH]),
                                        ALU.mult).then_inc(s_m, 1)

            def new_state(b, s, j, odd):
                q = NPAIR * (NB * b + s) + j
                if odd and j == NPAIR - 1 and s == NB - 1:
                    dve.wait_ge(s_st, 2 * q + 1)
                    dve.wait_ge(s_y, 2 * q + 1)
                    dve.wait_ge(s_sd, 2 * q + 1)
                    nc.vector.memset(xs[CH:P, 0, :], 0.0).then_inc(s_st, 1)
                    return
                dve.wait_ge(s_sd, 2 * q + odd + 1)
                dve.wait_ge(s_sps, q + 1)
                if odd:
                    dve.wait_ge(s_y, 2 * q + 1)
                    nc.vector.tensor_tensor(xs[CH:P, 0, :], xw[0:CH, :], wide[CH:P, 1, :], ALU.add).then_inc(s_st, 1)
                else:
                    nc.vector.tensor_tensor(xs[0:CH, 1, :], xw[CH:P, :], wide[0:CH, 1, :], ALU.add).then_inc(s_st, 1)

            def y_read(b, s, j, odd):
                q = NPAIR * (NB * b + s) + j
                dve.wait_ge(s_y, 2 * q + odd + 1)
                dve.wait_ge(s_dx, q + 1)
                gv = g[:, j, :, odd * CH:(odd + 1) * CH]
                nc.vector.tensor_tensor(gv, gv, ps_y[:], ALU.add).then_inc(s_yev, 1)

            def low_g(b, s, j):
                q = NPAIR * (NB * b + s) + j
                dve.wait_ge(s_ghi, q + 1)
                nc.vector.tensor_tensor(g_lo[:], g[:, j], g_hi[:].bitcast(F32), ALU.subtract).then_inc(s_glo, 1)

            def mean_square(b, s, j):
                q = NPAIR * (NB * b + s) + j
                dve.wait_ge(s_ss, q + 1)
                dve.wait_ge(s_rr, q)
                nc.vector.tensor_scalar(ms[:], ps_m[:, 0:1], 1.0 / DI, EPS, ALU.mult, ALU.add).then_inc(s_ms, 1)

            def finish(b, s, j):
                q = NPAIR * (NB * b + s) + j
                dve.wait_ge(s_o, q + 1)
                dve.wait_ge(s_rr, q + 1)
                dve.wait_ge(s_res[j], 16 * (NB * b + s + 1))
                nc.vector.scalar_tensor_tensor(out=res[:, j, :], in0=ring[:, bank(s, USE_O[j]), :], scalar=rr[:],
                                               in1=res[:, j, :], op0=ALU.mult, op1=ALU.add
                                               ).then_inc(s_out, 1)

            def body(b, s, n1, n2):
                nxt, nxt2 = ahead(b, s, 1), ahead(b, s, 2)
                x_read(b, s, 0)
                matrices(b, s, 0, 0)
                if n1:
                    steps(*nxt)
                y_read(b, s, 0, 0)
                matrices(b, s, 0, 1)
                new_state(b, s, 0, 0)
                if n1:
                    taps(*nxt, 0)
                new_state(b, s, 0, 1)
                if n2:
                    row_stats(*nxt2, 0)
                if n1:
                    sum_parts(*nxt)
                y_read(b, s, 0, 1)
                x_read(b, s, 1)
                matrices(b, s, 1, 0)
                if n2 and first:
                    normalise(*nxt2, 0)
                if n1:
                    step_weights(*nxt)
                low_g(b, s, 0)
                if n1:
                    taps(*nxt, 1)
                if n2 and first:
                    row_stats(*nxt2, 1)
                y_read(b, s, 1, 0)
                matrices(b, s, 1, 1)
                if n1:
                    stationary_sums(*nxt)
                new_state(b, s, 1, 0)
                if n2:
                    normalise(*nxt2, rounds - 1)
                new_state(b, s, 1, 1)
                mean_square(b, s, 0)
                y_read(b, s, 1, 1)
                finish(b, s, 0)
                if n1:
                    taps(*nxt, 2)
                    taps(*nxt, 3)
                low_g(b, s, 1)
                if n1:
                    taps(*nxt, 4)
                if n2:
                    split_u(*nxt2)
                mean_square(b, s, 1)
                finish(b, s, 1)

            def norm_all(b, s):
                for rnd in range(rounds):
                    row_stats(b, s, rnd)
                    normalise(b, s, rnd)

            norm_all(b0, 0)
            split_u(b0, 0)
            steps(b0, 0)
            taps(b0, 0, 0)
            sum_parts(b0, 0)
            step_weights(b0, 0)
            stationary_sums(b0, 0)
            norm_all(b0, 1)
            for c in range(1, NX + 1):
                taps(b0, 0, c)
            split_u(b0, 1)
            loop(dve, body)

        @block.gpsimd
        def _(pool):
            def inv_std(b, s, rnd):
                m = norm_round(NB * b + s, rnd)
                pool.wait_ge(s_mv, NPAIR * (m + 1))
                pool.wait_ge(s_norm, NPAIR * m)
                nc.gpsimd.tensor_tensor(rstd[:], mv[:, :, 1], const(K_EPS, 2), ALU.add).then_inc(s_var, 1)
                pool.wait_ge(s_var, m + 1)
                nc.gpsimd.tensor_tensor(rstd[:], rstd[:], const(K_HALF, 2), ALU.pow).then_inc(s_rstd, 1)

            def modulate(b, s):
                i = NB * b + s
                pool.wait_ge(s_mod, 16 * (b + 1))
                pool.wait_ge(s_norm, NPAIR * (2 * i + 1))
                for t in range(NPAIR):
                    h = hn[:, t, :]
                    nc.gpsimd.tensor_tensor(h, h, mod[:, 1, :], ALU.mult).then_inc(s_modm, 1)
                    pool.wait_ge(s_modm, NPAIR * i + t + 1)
                    nc.gpsimd.tensor_tensor(h, h, mod[:, 0, :], ALU.add).then_inc(s_moda, 1)

            def moving(b, s, c):
                n = 2 * NPAIR * (NB * b + s) + c
                pool.wait_ge(s_arg, n)
                if c == 0:
                    pool.wait_ge(s_vr, 3 * (NB * b + s + 1))
                nc.gpsimd.tensor_tensor(rhs[0:32], cum[0:32, s % 2, c * CH:(c + 1) * CH].unsqueeze(1)
                                        .broadcast_to([32, NH, CH]),
                                        const(K_DELTA, NH)[0:32].unsqueeze(2).broadcast_to([32, NH, CH]),
                                        ALU.mult).then_inc(s_rhs, 1)

            def diagonal(b, s, j):
                q = NPAIR * (NB * b + s) + j
                pool.wait_ge(s_mev, q + 1)
                pool.wait_ge(s_sps, q)
                nc.gpsimd.tensor_tensor(bd[:].rearrange("p (c n) -> p c n", c=2),
                                        misc[:, 0, :].unsqueeze(1).broadcast_to([P, 2, NS]),
                                        const(K_BLK, 2).unsqueeze(2).broadcast_to([P, 2, NS]),
                                        ALU.mult).then_inc(s_bd, 1)

            def skip_term(b, s, j):
                i = NB * b + s
                q = NPAIR * i + j
                pool.wait_ge(s_xc, NX * (i + 1))
                pool.wait_ge(s_ss, at_least_0(q - 1))
                nc.gpsimd.tensor_tensor(g[:, j], xc[:, :, j * P:(j + 1) * P],
                                        prm_sb[:, C_D:C_D + KI].unsqueeze(2).broadcast_to([P, KI, P]),
                                        ALU.mult).then_inc(s_dx, 1)

            def decay_state(b, s, j, odd):
                q = NPAIR * (NB * b + s) + j
                pool.wait_ge(s_dec, 2 * q + odd + 1)
                pool.wait_ge(s_st, 2 * q + odd)
                pool.wait_ge(s_sps, q + 1)
                nc.gpsimd.tensor_tensor(xw[:].rearrange("p (h n) -> p h n", n=NS),
                                        xs[:, odd, :].rearrange("p (h n) -> p h n", n=NS),
                                        dec[:, odd, :].unsqueeze(2).broadcast_to([P, NH, NS]),
                                        ALU.mult).then_inc(s_sd, 1)

            def gate(b, s, j):
                q = NPAIR * (NB * b + s) + j
                pool.wait_ge(s_yev, 2 * q + 2)
                if j == 0:
                    pool.wait_ge(s_zs, NB * b + s + 1)
                nc.gpsimd.tensor_tensor(g[:, j], g[:, j], zs[:, s % 2, :, j * P:(j + 1) * P], ALU.mult).then_inc(s_gate, 1)

            def squares(b, s, j):
                q = NPAIR * (NB * b + s) + j
                pool.wait_ge(s_sq, q + 1)
                for n, w in enumerate((4, 2, 1)):
                    if n:
                        pool.wait_ge(s_sum, 3 * q + n)
                    nc.gpsimd.tensor_tensor(g[:, j, 0:w], g[:, j, 0:w], g[:, j, w:2 * w], ALU.add).then_inc(s_sum, 1)

            def inv_rms(b, s, j):
                q = NPAIR * (NB * b + s) + j
                pool.wait_ge(s_ms, q + 1)
                pool.wait_ge(s_out, q)
                nc.gpsimd.tensor_tensor(rr[:], ms[:], const(K_HALF, 1), ALU.pow).then_inc(s_rr, 1)

            def body(b, s, n1, n2):
                nxt, nxt2 = ahead(b, s, 1), ahead(b, s, 2)
                diagonal(b, s, 0)
                moving(b, s, 1)
                skip_term(b, s, 0)
                decay_state(b, s, 0, 0)
                moving(b, s, 2)
                decay_state(b, s, 0, 1)
                if n2:
                    inv_std(*nxt2, 0)
                diagonal(b, s, 1)
                skip_term(b, s, 1)
                gate(b, s, 0)
                moving(b, s, 3)
                if n2 and first:
                    modulate(*nxt2)
                squares(b, s, 0)
                if n2 and first:
                    inv_std(*nxt2, 1)
                decay_state(b, s, 1, 0)
                decay_state(b, s, 1, 1)
                if n1:
                    moving(*nxt, 0)
                inv_rms(b, s, 0)
                gate(b, s, 1)
                squares(b, s, 1)
                inv_rms(b, s, 1)

            pool.wait_ge(s_cst, 32 * (layer + 1))
            pool.wait_ge(s_prm, 16 * (layer + 1))
            pool.wait_ge(s_init, 2 * (layer + 1))
            for s in range(2):
                if s:
                    moving(b0, 0, 0)
                for rnd in range(rounds):
                    inv_std(b0, s, rnd)
                    if first and rnd == 0:
                        modulate(b0, s)
            loop(pool, body)


def channel_mix(nc, sems, x_in, h_in, out, w3, prm, cst, mod_dram, mod_cols, nseq):
    T = 512
    NT = T // P
    halves = 2
    with ExitStack() as ctx:
        def sb(name, shape, dt=F32):
            return ctx.enter_context(nc.sbuf_tensor("f_" + name, shape, dt))

        def psum(name):
            return ctx.enter_context(nc.psum_tensor("f_" + name, [P, 2, 512], F32))

        def sem(name):
            return sems("f_" + name)

        w_hi = [sb(f"w_hi{n}", [P, KD, DM], F32R) for n in range(3)]
        w_lo = [sb(f"w_lo{n}", [P, KD, DM], F32R) for n in range(3)]
        prm_sb = sb("prm", [P, 2 * KD])
        small = sb("small", [P, NCST - K_ID])
        x_ld = sb("x_ld", [P, 2, NT, DM])
        h2 = sb("h2", [P, 2, NT, DM])
        x = sb("x", [P, 2, NT, DM])
        hn = sb("hn", [P, NT, DM])
        ht = sb("ht", [P, KD, T + 1])
        diff = sb("diff", [P, 2, T])
        mixed = sb("mixed", [P, 2, 2, T])
        r_hi, r_lo = sb("r_hi", [P, 2, KD, T], F32R), sb("r_lo", [P, 2, KD, T], F32R)
        k_hi, k_lo = sb("k_hi", [P, KD, T], F32R), sb("k_lo", [P, KD, T], F32R)
        kr, ka = sb("kr", [P, T]), sb("ka", [P, 2, T])
        ka_hi, ka_lo = sb("ka_hi", [P, KD, T], F32R), sb("ka_lo", [P, KD, T], F32R)
        rs = sb("rs", [P, NT, DM])
        gates = sb("gates", [P, 2, DM])
        spare = sb("spare", [P, 1])
        shift = sb("shift", [P, 2, KD])
        stats, mv, rstd = sb("stats", [P, NT, 6]), sb("mv", [P, NT, 2]), sb("rstd", [P, NT])
        ps_k, ps_r, ps_v, ps_t = psum("ps_k"), psum("ps_r"), psum("ps_v"), psum("ps_t")

        s_cst, s_stage, s_whi, s_wlo = sem("cst"), [sem("stage0"), sem("stage1")], sem("w_hi"), sem("w_lo")
        s_load, s_store = [sem("load0"), sem("load1")], [sem("store0"), sem("store1")]
        s_gal, s_gbl, s_shift = sem("ga_loaded"), sem("gb_loaded"), sem("shift")
        s_ga, s_x2 = sem("ga"), sem("x2")
        s_bn, s_mv, s_var, s_rstd, s_norm = sem("bn"), sem("mv"), sem("var"), sem("rstd"), sem("norm")
        s_t, s_ht, s_edge, s_diff, s_mix, s_mhi, s_mlo = (
            sem("t"), sem("ht"), sem("edge"), sem("diff"), sem("mix"), sem("m_hi"), sem("m_lo"))
        s_k, s_kr, s_ka, s_kahi, s_kalo = sem("k"), sem("kr"), sem("ka"), sem("ka_hi"), sem("ka_lo")
        s_r, s_rs, s_v, s_o, s_gb, s_y = sem("r"), sem("rs"), sem("v"), sem("o"), sem("gb"), sem("y")
        block = ctx.enter_context(nc.Block())

        ident = small[:, 0:P]
        stage = [hn[:].rearrange("p t d -> p (t d)"), rs[:].rearrange("p t d -> p (t d)")]

        def loop(eng, body):
            for s in range(halves):
                body(0, s, False)
            with eng.Fori(1, nseq - 1) as b:
                for s in range(halves):
                    body(b, s, False)
            for s in range(halves):
                body(nseq - 1, s, s == halves - 1)

        def at_least_0(count):
            return max(count, 0) if isinstance(count, int) else count

        def mixed_high(s, m):
            return k_hi if m else r_hi[:, s]

        def mixed_low(s, m):
            return k_lo if m else r_lo[:, s]

        def after(b, s):
            return (b + 1, 0) if s == halves - 1 else (b, s + 1)

        @block.sync
        def _(sp):
            sp.dma_start(small[:], cst[:, K_ID:NCST]).then_inc(s_cst, 16)
            sp.dma_start(prm_sb[:], prm).then_inc(s_cst, 16)

            def load(b, s):
                i = halves * b + s
                sp.wait_ge(s_x2, at_least_0(NT * (i - 1)))
                for src, to in ((x_in, x_ld), (h_in, h2)):
                    sp.dma_start(to[:, s], src[bass.ds(i * T, T), :].rearrange("(t p) d -> p t d", p=P)
                                 ).then_inc(s_load[s], 16)

            for n in range(3):
                if n == 2:
                    sp.wait_ge(s_wlo, 1)
                sp.dma_start(stage[n % 2], w3[n].rearrange("p k n -> p (k n)")).then_inc(s_stage[n % 2], 16)

            def load_shift(b):
                sp.wait_ge(s_ht, halves * KD * b)
                sp.dma_start(shift[:], mod_cols[bass.ds(b, 1)].rearrange("o p (s k) -> (o p) s k", s=2)
                             ).then_inc(s_shift, 16)

            def load_ga(b):
                sp.wait_ge(s_ga, halves * NT * b)
                sp.dma_start(gates[:, 0, :], mod_dram[bass.ds(b, 1), 2 * DM:3 * DM].broadcast_to([P, DM])
                             ).then_inc(s_gal, 16)

            def load_gb(b):
                sp.wait_ge(s_gb, halves * NT * b)
                sp.dma_start(gates[:, 1, :], mod_dram[bass.ds(b, 1), 5 * DM:6 * DM].broadcast_to([P, DM])
                             ).then_inc(s_gbl, 16)

            load_shift(0)
            load_ga(0)
            load_gb(0)
            load(0, 0)
            load(0, 1)

            def body(b, s, end):
                i = halves * b + s
                more = not (isinstance(b, int) and b == nseq - 1)
                if more:
                    load(b + 1, s)
                    if s == 0:
                        load_ga(b + 1)
                        load_shift(b + 1)
                for t in range(NT):
                    sp.wait_ge(s_y, NT * i + t + 1)
                    sp.dma_start(out[bass.ds(i * T + t * P, P), :], x[:, s, t, :]).then_inc(s_store[s], 16)
                if more and s:
                    load_gb(b + 1)

            loop(sp, body)
            for k in range(2):
                sp.wait_ge(s_store[k], 16 * NT * nseq)

        @block.tensor
        def _(pe):
            def products(out_ps, parts):
                n, k = 3 * len(parts), 0
                for (a_hi, a_lo), (b_hi, b_lo) in parts:
                    for a, c in ((a_lo, b_hi), (a_hi, b_lo), (a_hi, b_hi)):
                        last = nc.tensor.matmul(out_ps, a, c, start=(k == 0), stop=(k == n - 1))
                        k += 1
                return last

            def bank_free(sem_read, i, m):
                pe.wait_ge(sem_read, 4 * i + m - 1 if m >= 2 else 4 * i)

            def turn(b, s):
                i = halves * b + s
                pe.wait_ge(s_norm, NT * (i + 1))
                for d in range(KD):
                    bank_free(s_ht, i, d)
                    for t in range(NT):
                        last = nc.tensor.transpose(ps_t[:, d % 2, t * P:(t + 1) * P], hn[:, t, d * P:(d + 1) * P],
                                                   ident)
                    last.then_inc(s_t, 1)

            pe.wait_ge(s_cst, 32)
            pe.wait_ge(s_wlo, 3)
            turn(0, 0)

            def body(b, s, end):
                i = halves * b + s
                pe.wait_ge(s_mlo, 2 * KD * (i + 1))
                for m in range(KD):
                    bank_free(s_kr, i, m)
                    c = slice(m * P, (m + 1) * P)
                    products(ps_k[:, m % 2, :], [((w_hi[1][:, k, c], w_lo[1][:, k, c]), (k_hi[:, k, :], k_lo[:, k, :]))
                                                 for k in range(KD)]).then_inc(s_k, 1)
                for t in range(NT):
                    if t == 2 and not end:
                        turn(*after(b, s))
                    bank_free(s_rs, i, t)
                    c = slice(t * P, (t + 1) * P)
                    products(ps_r[:, t % 2, :], [((r_hi[:, s, k, c], r_lo[:, s, k, c]),
                                                  (w_hi[0][:, k, :], w_lo[0][:, k, :])) for k in range(KD)]
                             ).then_inc(s_r, 1)
                pe.wait_ge(s_kalo, KD * (i + 1))
                for t in range(NT):
                    bank_free(s_o, i, t)
                    c = slice(t * P, (t + 1) * P)
                    products(ps_v[:, t % 2, :], [((ka_hi[:, k, c], ka_lo[:, k, c]),
                                                  (w_hi[2][:, k, :], w_lo[2][:, k, :])) for k in range(KD)]
                             ).then_inc(s_v, 1)

            loop(pe, body)

        @block.scalar
        def _(act):
            for n in range(3):
                act.wait_ge(s_stage[n % 2], 16 * (n // 2 + 1))
                nc.scalar.activation(w_hi[n][:].rearrange("p k n -> p (k n)"), stage[n % 2], ACT.Identity
                                     ).then_inc(s_whi, 1)

            def affine(b, s, between=()):
                i = halves * b + s
                act.wait_ge(s_shift, 16 * (b + 1))
                act.wait_ge(s_mix, 2 * KD * i)
                if s == 0:
                    nc.scalar.mul(ht[:, :, 0:1], ident[:, 0:KD].unsqueeze(2), 0.0).then_inc(s_edge, 1)
                else:
                    act.wait_ge(s_ht, KD * i)
                    nc.scalar.copy(ht[:, :, 0:1], ht[:, :, T:T + 1]).then_inc(s_edge, 1)
                act.wait_ge(s_edge, i + 1)
                for d in range(KD):
                    act.wait_ge(s_t, KD * i + d + 1)
                    nc.scalar.activation(ht[:, d, 1:], ps_t[:, d % 2, :], ACT.Identity,
                                         bias=shift[:, 0, d:d + 1], scale=shift[:, 1, d:d + 1]).then_inc(s_ht, 1)
                    if d:
                        high(b, s, d - 1)
                    if d >= 2:
                        for step in between[d - 2:d - 1]:
                            step()
                high(b, s, KD - 1)

            def high(b, s, d):
                i = halves * b + s
                for m in range(2):
                    n = 2 * (KD * i + d) + m
                    act.wait_ge(s_mix, n + 1)
                    nc.scalar.activation(mixed_high(s, m)[:, d, :], mixed[:, d % 2, m, :], ACT.Identity
                                         ).then_inc(s_mhi, 1)

            def receptance(b, s, t):
                i = halves * b + s
                act.wait_ge(s_r, NT * i + t + 1)
                if t == 0:
                    act.wait_ge(s_y, NT * i)
                nc.scalar.activation(rs[:, t, :], ps_r[:, t % 2, :], ACT.Sigmoid).then_inc(s_rs, 1)

            def relu(b, s, m):
                n = KD * (halves * b + s) + m
                act.wait_ge(s_k, n + 1)
                act.wait_ge(s_ka, n)
                nc.scalar.activation(kr[:], ps_k[:, m % 2, :], ACT.Relu).then_inc(s_kr, 1)

            def high_k(b, s, m):
                i = halves * b + s
                act.wait_ge(s_ka, KD * i + m + 1)
                if m == 0:
                    act.wait_ge(s_v, NT * i)
                nc.scalar.activation(ka_hi[:, m, :], ka[:, m % 2, :], ACT.Identity).then_inc(s_kahi, 1)

            affine(0, 0)

            def body(b, s, end):
                for m in range(KD):
                    relu(b, s, m)
                    if m:
                        high_k(b, s, m - 1)
                high_k(b, s, KD - 1)
                receptance(b, s, 0)
                receptance(b, s, 1)
                if end:
                    receptance(b, s, 2)
                    receptance(b, s, 3)
                else:
                    affine(*after(b, s), [lambda: receptance(b, s, 2), lambda: receptance(b, s, 3)])

            loop(act, body)

        @block.vector
        def _(dve):
            dve.wait_ge(s_cst, 32)
            for n in range(3):
                dve.wait_ge(s_whi, n + 1)
                nc.vector.tensor_tensor(w_lo[n][:].rearrange("p k n -> p (k n)"), stage[n % 2],
                                        w_hi[n][:].rearrange("p k n -> p (k n)").bitcast(F32), ALU.subtract
                                        ).then_inc(s_wlo, 1)

            def norm(b, s):
                i = halves * b + s
                dve.wait_ge(s_mv, NT * i)
                dve.wait_ge(s_norm, NT * i)
                for t in range(NT):
                    dve.wait_ge(s_x2, NT * i + t + 1)
                    nc.vector.bn_stats(stats[:, t, :], x[:, s, t, :]).then_inc(s_bn, 1)
                dve.wait_ge(s_bn, NT * (i + 1))
                nc.vector.memset(spare[:], 0.0)
                for t in range(NT):
                    nc.vector.bn_aggr(mv[:, t, :], stats[:, t, :]).then_inc(s_mv, 1)
                dve.wait_ge(s_rstd, i + 1)
                dve.wait_ge(s_t, KD * i)
                for t in range(NT):
                    nc.vector.tensor_scalar(hn[:, t, :], x[:, s, t, :], mv[:, t, 0:1], rstd[:, t:t + 1],
                                            ALU.subtract, ALU.mult).then_inc(s_norm, 1)

            def mix(b, s, d):
                n = KD * (halves * b + s) + d
                dve.wait_ge(s_ht, n + 1)
                dve.wait_ge(s_mix, at_least_0(2 * (n - 1)))
                nc.vector.tensor_tensor(diff[:, d % 2, :], ht[:, d, 1:], ht[:, d, 0:T], ALU.subtract
                                        ).then_inc(s_diff, 1)
                dve.wait_ge(s_mlo, at_least_0(2 * (n - 1)))
                dve.wait_ge(s_diff, n + 1)
                for m in range(2):
                    mu = prm_sb[:, m * KD + d:m * KD + d + 1]
                    nc.vector.scalar_tensor_tensor(out=mixed[:, d % 2, m, :], in0=diff[:, d % 2, :], scalar=mu,
                                                   in1=ht[:, d, 0:T], op0=ALU.mult, op1=ALU.add
                                                   ).then_inc(s_mix, 1)

            def mixed_rest(b, s, d):
                n = KD * (halves * b + s) + d
                for m in range(2):
                    dve.wait_ge(s_mhi, 2 * n + m + 1)
                    nc.vector.tensor_tensor(mixed_low(s, m)[:, d, :], mixed[:, d % 2, m, :],
                                            mixed_high(s, m)[:, d, :].bitcast(F32), ALU.subtract).then_inc(s_mlo, 1)

            def square(b, s, m):
                i = halves * b + s
                dve.wait_ge(s_kr, KD * i + m + 1)
                dve.wait_ge(s_kalo, at_least_0(KD * i + m - 1))
                nc.vector.tensor_tensor(ka[:, m % 2, :], kr[:], kr[:], ALU.mult).then_inc(s_ka, 1)

            def square_rest(b, s, m):
                dve.wait_ge(s_kahi, KD * (halves * b + s) + m + 1)
                nc.vector.tensor_tensor(ka_lo[:, m, :], ka[:, m % 2, :], ka_hi[:, m, :].bitcast(F32), ALU.subtract
                                        ).then_inc(s_kalo, 1)

            def gate_v(b, s, t):
                i = halves * b + s
                dve.wait_ge(s_v, NT * i + t + 1)
                dve.wait_ge(s_rs, NT * i + t + 1)
                nc.vector.tensor_tensor(rs[:, t, :], rs[:, t, :], ps_v[:, t % 2, :], ALU.mult).then_inc(s_o, 1)

            norm(0, 0)
            for d in range(KD):
                mix(0, 0, d)
                mixed_rest(0, 0, d)

            def body(b, s, end):
                for m in range(KD):
                    square(b, s, m)
                    if m:
                        square_rest(b, s, m - 1)
                square_rest(b, s, KD - 1)
                if end:
                    for t in range(NT):
                        gate_v(b, s, t)
                    return
                nxt = after(b, s)
                norm(*nxt)
                mix(*nxt, 0)
                mix(*nxt, 1)
                mixed_rest(*nxt, 0)
                mix(*nxt, 2)
                mixed_rest(*nxt, 1)
                gate_v(b, s, 0)
                mix(*nxt, 3)
                mixed_rest(*nxt, 2)
                gate_v(b, s, 1)
                mixed_rest(*nxt, 3)
                gate_v(b, s, 2)
                gate_v(b, s, 3)

            loop(dve, body)

        @block.gpsimd
        def _(pool):
            pool.wait_ge(s_cst, 32)

            def residual(b, s):
                i = halves * b + s
                pool.wait_ge(s_gal, 16 * (b + 1))
                pool.wait_ge(s_load[s], 32 * (b + 1))
                for t in range(NT):
                    nc.gpsimd.tensor_tensor(h2[:, s, t, :], h2[:, s, t, :], gates[:, 0, :], ALU.mult
                                            ).then_inc(s_ga, 1)
                    if t == 0:
                        pool.wait_ge(s_store[s], 16 * NT * b)
                    pool.wait_ge(s_ga, NT * i + t + 1)
                    nc.gpsimd.tensor_tensor(x[:, s, t, :], x_ld[:, s, t, :], h2[:, s, t, :], ALU.add
                                            ).then_inc(s_x2, 1)

            def inv_std(b, s):
                i = halves * b + s
                pool.wait_ge(s_mv, NT * (i + 1))
                pool.wait_ge(s_norm, NT * i)
                eps = small[:, K_EPS - K_ID:K_EPS - K_ID + 1].broadcast_to([P, NT])
                half = small[:, K_HALF - K_ID:K_HALF - K_ID + 1].broadcast_to([P, NT])
                nc.gpsimd.tensor_tensor(rstd[:], mv[:, :, 1], eps, ALU.add).then_inc(s_var, 1)
                pool.wait_ge(s_var, i + 1)
                nc.gpsimd.tensor_tensor(rstd[:], rstd[:], half, ALU.pow).then_inc(s_rstd, 1)

            residual(0, 0)
            inv_std(0, 0)

            def body(b, s, end):
                i = halves * b + s
                if not end:
                    residual(*after(b, s))
                    inv_std(*after(b, s))
                pool.wait_ge(s_gbl, 16 * (b + 1))
                for t in range(NT):
                    pool.wait_ge(s_o, NT * i + t + 1)
                    nc.gpsimd.tensor_tensor(rs[:, t, :], rs[:, t, :], gates[:, 1, :], ALU.mult
                                            ).then_inc(s_gb, 1)
                    pool.wait_ge(s_gb, NT * i + t + 1)
                    nc.gpsimd.tensor_tensor(x[:, s, t, :], x[:, s, t, :], rs[:, t, :], ALU.add).then_inc(s_y, 1)

            loop(pool, body)


def build(nc, x, in_w, out_w, prm, w3, fprm, cT, wmod, cst, out, nseq):
    rows = x.shape[0]
    mod_dram = nc.dram_tensor("mod_scratch", [nseq, 6 * DM], F32, kind="Internal").ap()
    h1 = nc.dram_tensor("h1_scratch", [rows, DM], F32, kind="Internal").ap()
    h2 = nc.dram_tensor("h2_scratch", [rows, DM], F32, kind="Internal").ap()
    mod_cols = nc.dram_tensor("mod_cols_scratch", [nseq, P, 2 * KD], F32, kind="Internal").ap()
    with ExitStack() as ctx:
        known = {}

        def sems(name):
            if name not in known:
                known[name] = ctx.enter_context(nc.semaphore(name))
            return known[name]

        modulation(nc, sems, cT, wmod, cst, mod_dram, mod_cols, nseq)
        mamba_layer(nc, sems, 0, x, h1, in_w[0], out_w[0], prm[0], cst, mod_dram, nseq)
        mamba_layer(nc, sems, 1, h1, h2, in_w[1], out_w[1], prm[1], cst, mod_dram, nseq)
        channel_mix(nc, sems, x, h2, out, w3, fprm, cst, mod_dram, mod_cols, nseq)


def layout(inputs):
    g = {k: np.ascontiguousarray(v) for k, v in inputs.items()}

    def tiles(w):
        return w.reshape(w.shape[0] // P, P, w.shape[1]).transpose(1, 0, 2)

    def cols(vec):
        return vec.reshape(-1, P).T

    in_w, out_w, prm = [], [], []
    for n in range(NL):
        w = g["L0_attn_in_proj_w"][n]
        z, xx, bc, dt = w[:DI], w[DI:2 * DI], w[2 * DI:2 * DI + 2 * NS], w[2 * DI + 2 * NS:]
        order = [dt] * (P // NH) + [bc]
        for k in range(1, NG):
            part, c = (z, Z_AT.index(k)) if k in Z_AT else (xx, X_AT.index(k))
            order.append(part[c * 2 * P:(c + 1) * 2 * P])
        in_w.append(tiles(np.concatenate(order).T))
        out_w.append(tiles(g["L0_attn_out_proj_w"][n].T))
        cw, cb = g["L0_attn_conv_w"][n], g["L0_attn_conv_b"][n]
        cw = np.concatenate([cw[DI:], cw[:DI]]).reshape(9, P, TAPS).transpose(1, 0, 2).reshape(P, 9 * TAPS)
        cb = cols(np.concatenate([cb[DI:], cb[:DI]]))
        rep = P // NH
        prm.append(np.concatenate([
            cw, cb, cols(np.repeat(g["L0_attn_D"][n], NS)), cols(g["L0_attn_rms_w"][n]),
            cols(g["L0_attn_ln_w"][n]), cols(g["L0_attn_ln_b"][n]),
            np.tile(g["L0_attn_A_log"][n], rep)[:, None], np.tile(g["L0_attn_dt_bias"][n], rep)[:, None]], axis=1))
    x = g["L0_attn_x"]
    return {
        "x": x.reshape(-1, DM),
        "in_w": np.stack(in_w), "out_w": np.stack(out_w), "prm": np.stack(prm),
        "w3": np.stack([tiles(g[k].T) for k in ("L0_ffn_W_r", "L0_ffn_W_k", "L0_ffn_W_v")]),
        "fprm": np.concatenate([cols(g["L0_ffn_mu_r"]), cols(g["L0_ffn_mu_k"])], axis=1),
        "cT": g["L0_c"].T.reshape(KD, P, -1).transpose(1, 0, 2),
        "wmod": tiles(g["L0_wmod"]),
        "cst": shape_constants(),
    }


def kernel(**inputs):
    import concourse.bacc as _bacc
    from concourse import mybir as _mybir
    from concourse.bass_utils import run_bass_kernel_spmd as _run

    nc = _bacc.Bacc("TRN2", target_bir_lowering=False, num_devices=1)
    arrays, args = {}, []
    for name, a in layout(inputs).items():
        a = np.ascontiguousarray(a)
        arrays[f"in_{name}"] = a
        args.append(nc.dram_tensor(f"in_{name}", a.shape, _mybir.dt.from_np(a.dtype), kind="ExternalInput").ap())
    shape = inputs["L0_attn_x"].shape
    args.append(nc.dram_tensor("out_0", (shape[0] * shape[1], DM), F32, kind="ExternalOutput").ap())
    build(nc, *args, shape[0])
    r = _run(nc, [arrays], core_ids=[0])
    return r.results[0]["out_0"].reshape(shape)
```
